# Optimizing a Trainium2 kernel written in Bass

```python
import numpy as np
import jax
import jax.numpy as jnp

def _softmax(x, axis=-1):
    return jax.nn.softmax(x, axis=axis)

def _gelu(x):
    return jax.nn.gelu(x, approximate=True)

def _silu(x):
    return jax.nn.silu(x)

def _sigmoid(x):
    return jax.nn.sigmoid(x)

def _layernorm(x, axis=-1, eps=1e-05):
    m = jnp.mean(x, axis=axis, keepdims=True)
    v = jnp.var(x, axis=axis, keepdims=True)
    return (x - m) / jnp.sqrt(v + eps)

def _scatter_add(tgt, idx, src, axis=0):
    return tgt.at[idx].add(src)

def _segment_sum(src, seg, n):
    return jax.ops.segment_sum(src, seg, n)
kernel_name = 'mk_seq_postln_d2_jaxref_r8_543aa2'

def setup_inputs(seed: int=0):
    np.random.seed(seed)
    _w = jnp.asarray

    def _L0_attn_setup():
        import jax, jax.numpy as jnp
        import numpy as np
        B, S, D = (4, 256, 128)

        def _gaussian_mask(seq_len, dtype):
            pos = jnp.arange(seq_len, dtype=dtype)
            center = seq_len / 2
            sigma = seq_len / 4
            m = jnp.exp(-0.5 * ((pos - center) / sigma) ** 2)
            return m[None, None, :]
        key = jax.random.key(seed)
        ks = jax.random.split(key, 9)
        sc = 1.0 / np.sqrt(D)
        return {'x': jax.random.normal(ks[0], (B, S, D), dtype=jnp.float32), 'Wq': jax.random.normal(ks[1], (D, D), dtype=jnp.float32) * sc, 'bq': jnp.zeros((D,), dtype=jnp.float32), 'Wk': jax.random.normal(ks[2], (D, D), dtype=jnp.float32) * sc, 'bk': jnp.zeros((D,), dtype=jnp.float32), 'Wv': jax.random.normal(ks[3], (D, D), dtype=jnp.float32) * sc, 'bv': jnp.zeros((D,), dtype=jnp.float32), 'Wo': jax.random.normal(ks[4], (D, D), dtype=jnp.float32) * sc, 'bo': jnp.zeros((D,), dtype=jnp.float32)}
    _L0_attn_in = _L0_attn_setup()

    def _L0_ffn_setup():
        import jax, jax.numpy as jnp
        import numpy as np
        B, S, H, F, E, K = (4, 256, 128, 448, 8, 2)
        CAP_FACTOR = 1.25

        def _moe_forward(hidden_states, gate_w, w1, w2, w3):
            b, s, h = hidden_states.shape
            dtype = hidden_states.dtype
            x = hidden_states.reshape(-1, h)
            router_logits = x @ gate_w.T
            expert_weights = jax.nn.softmax(router_logits.astype(jnp.float32), axis=1)
            _, selected_experts = jax.lax.top_k(expert_weights, K)
            top_k_idx = selected_experts.reshape(b, s, K)
            probs = expert_weights.reshape(b, s, E)
            capacity = int(s * K / E * CAP_FACTOR)
            expert_mask = jax.nn.one_hot(top_k_idx, E, dtype=jnp.int32)
            mask_fused = expert_mask.reshape(b, s * K, E)
            count_fused = jnp.cumsum(mask_fused, axis=1)
            count = count_fused.reshape(b, s, K, E)
            trunc_mask = expert_mask * (count <= capacity).astype(jnp.int32)
            combined_mask = trunc_mask.sum(axis=2)
            masked_probs = probs * combined_mask
            pos_fused = mask_fused * count_fused
            pos = pos_fused.reshape(b, s, K, E)
            combined_pos = pos.sum(axis=2) * combined_mask
            pos_in_cap = jax.nn.one_hot(combined_pos, capacity + 1, dtype=jnp.int32)
            combine_mask = masked_probs[..., None] * pos_in_cap
            combine_mask = combine_mask[..., 1:].astype(dtype)
            dispatch_mask = (combine_mask != 0).astype(dtype)
            dispatch = jnp.einsum('bsm,bsec->ebcm', hidden_states, dispatch_mask)
            h1 = jnp.einsum('ebcm,emh->ebch', dispatch, w1)
            h3 = jnp.einsum('ebcm,emh->ebch', dispatch, w3)
            expert_out = jnp.einsum('ebch,ehm->ebcm', jax.nn.silu(h1) * h3, w2)
            final = jnp.einsum('ebcm,bsec->bsm', expert_out, combine_mask)
            return final
        key = jax.random.key(seed)
        k1, k2, k3, k4, k5 = jax.random.split(key, 5)
        s_h = 1.0 / np.sqrt(H)
        s_f = 1.0 / np.sqrt(F)
        return {'hidden_states': jax.random.normal(k1, (B, S, H), dtype=jnp.float32), 'gate_w': jax.random.normal(k2, (E, H), dtype=jnp.float32) * s_h, 'w1': jax.random.normal(k3, (E, H, F), dtype=jnp.float32) * s_h, 'w2': jax.random.normal(k4, (E, F, H), dtype=jnp.float32) * s_f, 'w3': jax.random.normal(k5, (E, H, F), dtype=jnp.float32) * s_h}
    _L0_ffn_in = _L0_ffn_setup()

    def _L1_attn_setup():
        import jax, jax.numpy as jnp
        import numpy as np
        DIM = 128
        SQRT_DIM = float(np.sqrt(DIM))
        key = jax.random.key(seed)
        inputs = jax.random.normal(key, (512, 4, DIM), dtype=jnp.float32)
        return {'inputs': inputs}
    _L1_attn_in = _L1_attn_setup()

    def _L1_ffn_setup():
        import jax, jax.numpy as jnp
        import numpy as np
        D_MODEL, D_FF, RANK = (128, 512, 32)
        B, S = (4, 512)
        key = jax.random.key(seed)
        ks = jax.random.split(key, 7)
        return {'x': jax.random.normal(ks[0], (B, S, D_MODEL), dtype=jnp.float32), 'U1': jax.random.normal(ks[1], (D_MODEL, RANK), dtype=jnp.float32) * 0.02, 'V1': jax.random.normal(ks[2], (RANK, D_FF), dtype=jnp.float32) * 0.02, 'b1': jnp.zeros((D_FF,), dtype=jnp.float32), 'U2': jax.random.normal(ks[3], (D_FF, RANK), dtype=jnp.float32) * 0.02, 'V2': jax.random.normal(ks[4], (RANK, D_MODEL), dtype=jnp.float32) * 0.02, 'b2': jnp.zeros((D_MODEL,), dtype=jnp.float32)}
    _L1_ffn_in = _L1_ffn_setup()
    _d = {'L0_attn_x': _L0_attn_in['x'], 'L0_attn_Wq': _L0_attn_in['Wq'], 'L0_attn_bq': _L0_attn_in['bq'], 'L0_attn_Wk': _L0_attn_in['Wk'], 'L0_attn_bk': _L0_attn_in['bk'], 'L0_attn_Wv': _L0_attn_in['Wv'], 'L0_attn_bv': _L0_attn_in['bv'], 'L0_attn_Wo': _L0_attn_in['Wo'], 'L0_attn_bo': _L0_attn_in['bo'], 'L0_ffn_gate_w': _L0_ffn_in['gate_w'], 'L0_ffn_w1': _L0_ffn_in['w1'], 'L0_ffn_w2': _L0_ffn_in['w2'], 'L0_ffn_w3': _L0_ffn_in['w3'], 'L1_ffn_U1': _L1_ffn_in['U1'], 'L1_ffn_V1': _L1_ffn_in['V1'], 'L1_ffn_b1': _L1_ffn_in['b1'], 'L1_ffn_U2': _L1_ffn_in['U2'], 'L1_ffn_V2': _L1_ffn_in['V2'], 'L1_ffn_b2': _L1_ffn_in['b2']}
    _x0 = _d['L0_attn_x']
    _d['L0_attn_x'] = jax.random.normal(jax.random.fold_in(jax.random.key(seed), 1), (4, 1024, 128), dtype=_x0.dtype)
    del _x0
    return _d

def reference(L0_attn_x, L0_attn_Wq, L0_attn_bq, L0_attn_Wk, L0_attn_bk, L0_attn_Wv, L0_attn_bv, L0_attn_Wo, L0_attn_bo, L0_ffn_gate_w, L0_ffn_w1, L0_ffn_w2, L0_ffn_w3, L1_ffn_U1, L1_ffn_V1, L1_ffn_b1, L1_ffn_U2, L1_ffn_V2, L1_ffn_b2):

    def _L0_attn_ref(x, Wq, bq, Wk, bk, Wv, bv, Wo, bo):
        import jax, jax.numpy as jnp
        import numpy as np
        B, S, D = (4, 256, 128)

        def _gaussian_mask(seq_len, dtype):
            pos = jnp.arange(seq_len, dtype=dtype)
            center = seq_len / 2
            sigma = seq_len / 4
            m = jnp.exp(-0.5 * ((pos - center) / sigma) ** 2)
            return m[None, None, :]
        d = x.shape[-1]
        Q = x @ Wq.T + bq
        K = x @ Wk.T + bk
        V = x @ Wv.T + bv
        scores = jnp.einsum('bqd,bkd->bqk', Q, K) / jnp.sqrt(jnp.asarray(d, x.dtype))
        scores = scores * _gaussian_mask(x.shape[1], x.dtype)
        attn = jax.nn.softmax(scores, axis=-1)
        out = jnp.einsum('bqk,bkd->bqd', attn, V)
        return out @ Wo.T + bo

    def _L0_ffn_ref(hidden_states, gate_w, w1, w2, w3):
        import jax, jax.numpy as jnp
        import numpy as np
        B, S, H, F, E, K = (4, 256, 128, 448, 8, 2)
        CAP_FACTOR = 1.25

        def _moe_forward(hidden_states, gate_w, w1, w2, w3):
            b, s, h = hidden_states.shape
            dtype = hidden_states.dtype
            x = hidden_states.reshape(-1, h)
            router_logits = x @ gate_w.T
            expert_weights = jax.nn.softmax(router_logits.astype(jnp.float32), axis=1)
            _, selected_experts = jax.lax.top_k(expert_weights, K)
            top_k_idx = selected_experts.reshape(b, s, K)
            probs = expert_weights.reshape(b, s, E)
            capacity = int(s * K / E * CAP_FACTOR)
            expert_mask = jax.nn.one_hot(top_k_idx, E, dtype=jnp.int32)
            mask_fused = expert_mask.reshape(b, s * K, E)
            count_fused = jnp.cumsum(mask_fused, axis=1)
            count = count_fused.reshape(b, s, K, E)
            trunc_mask = expert_mask * (count <= capacity).astype(jnp.int32)
            combined_mask = trunc_mask.sum(axis=2)
            masked_probs = probs * combined_mask
            pos_fused = mask_fused * count_fused
            pos = pos_fused.reshape(b, s, K, E)
            combined_pos = pos.sum(axis=2) * combined_mask
            pos_in_cap = jax.nn.one_hot(combined_pos, capacity + 1, dtype=jnp.int32)
            combine_mask = masked_probs[..., None] * pos_in_cap
            combine_mask = combine_mask[..., 1:].astype(dtype)
            dispatch_mask = (combine_mask != 0).astype(dtype)
            dispatch = jnp.einsum('bsm,bsec->ebcm', hidden_states, dispatch_mask)
            h1 = jnp.einsum('ebcm,emh->ebch', dispatch, w1)
            h3 = jnp.einsum('ebcm,emh->ebch', dispatch, w3)
            expert_out = jnp.einsum('ebch,ehm->ebcm', jax.nn.silu(h1) * h3, w2)
            final = jnp.einsum('ebcm,bsec->bsm', expert_out, combine_mask)
            return final
        return _moe_forward(hidden_states, gate_w, w1, w2, w3)

    def _L1_attn_ref(inputs):
        import jax, jax.numpy as jnp
        import numpy as np
        DIM = 128
        SQRT_DIM = float(np.sqrt(DIM))
        x = jnp.transpose(inputs, (1, 0, 2))
        scores = jnp.einsum('bsd,btd->bst', x, x) / SQRT_DIM
        attn = jax.nn.softmax(scores, axis=-1)
        out = jnp.einsum('bst,btd->bsd', attn, x)
        return jnp.transpose(out, (1, 0, 2))

    def _L1_ffn_ref(x, U1, V1, b1, U2, V2, b2):
        import jax, jax.numpy as jnp
        import numpy as np
        D_MODEL, D_FF, RANK = (128, 512, 32)
        B, S = (4, 512)
        P = jnp.einsum('bsd,dr->bsr', x, U1)
        H = jax.nn.gelu(jnp.einsum('bsr,rf->bsf', P, V1) + b1)
        Q = jnp.einsum('bsf,fr->bsr', H, U2)
        return jnp.einsum('bsr,rd->bsd', Q, V2) + b2
    x = L0_attn_x
    x = _layernorm(x + _L0_attn_ref(x, L0_attn_Wq, L0_attn_bq, L0_attn_Wk, L0_attn_bk, L0_attn_Wv, L0_attn_bv, L0_attn_Wo, L0_attn_bo), axis=-1)
    x = _layernorm(x + _L0_ffn_ref(x, L0_ffn_gate_w, L0_ffn_w1, L0_ffn_w2, L0_ffn_w3), axis=-1)
    x = _layernorm(x + _L1_attn_ref(x), axis=-1)
    x = _layernorm(x + _L1_ffn_ref(x, L1_ffn_U1, L1_ffn_V1, L1_ffn_b1, L1_ffn_U2, L1_ffn_V2, L1_ffn_b2), axis=-1)
    return x

_drawn_inputs = setup_inputs


def setup_inputs(seed=0):
    import zlib

    import numpy as np

    out = dict(_drawn_inputs(seed))
    spreads = {'L0_attn_bq': (0.0, 0.606),
     'L0_attn_bk': (0.0, 2.0),
     'L0_attn_bv': (0.0, 0.1),
     'L0_attn_bo': (0.0, 0.1),
     'L1_ffn_b1': (0.0, 0.8),
     'L1_ffn_b2': (0.0, 0.306)}
    factors = {'L1_ffn_U1': 8.0, 'L1_ffn_V1': 8.0, 'L1_ffn_U2': 8.0, 'L1_ffn_V2': 8.0}
    for name, (base, spread) in spreads.items():
        noise = np.random.default_rng([zlib.crc32(name.encode()), seed]).standard_normal(out[name].shape)
        drawn = base * np.exp(spread * noise) if base else spread * noise
        out[name] = jnp.asarray(drawn.astype(out[name].dtype))
    for name, factor in factors.items():
        out[name] = (out[name] * factor).astype(out[name].dtype)
    return out
```

```python
from contextlib import ExitStack

import numpy as np

import concourse.bass as bass
from concourse import mybir

F32 = mybir.dt.float32
U32 = mybir.dt.uint32
ALU = mybir.AluOpType
ACT = mybir.ActivationFunctionType
AX = mybir.AxisListType

P = 128
B, S, D = 4, 1024, 128
E, K, F = 8, 2, 448
CAP = int(S * K / E * 1.25)
DFF, RANK = 512, 32
EPS = 1e-5
T = S // P
NT = B * T
PAIRS = B // 2
SLOTS = 2 * CAP
Q = SLOTS // P
J = PAIRS * E
ROWS = J * SLOTS
FT = F - 3 * P
HALF = SLOTS // 2
NU = 8
SUB = 32
NJ = P // SUB
FC = DFF // P

C_ID, C_TRI, C_ONE, C_BLK = 0, P, 2 * P, 3 * P
C_BASE = 4 * P
C_TRASH = C_BASE + B * K * T
C_IOTA = C_TRASH + B * K * T
C_END = C_IOTA + E


class Steps:

    def __init__(self, eng, sem):
        self.eng, self.sem, self.n = eng, sem, 0

    def add(self, ins):
        ins.then_inc(self.sem, 1)
        self.n += 1

    def wait(self, back=0):
        self.eng.wait_ge(self.sem, self.n - back)

    def close(self):
        self.wait()
        self.eng.sem_clear(self.sem)
        self.n = 0


def build(nc, xT, x, wqT, wkT, wv, woT, bq, bk, bv, bo, gateT, w13, w2, u1T, v1, u2T, v2, b1, b2, consts, gmask, out):
    ctx = ExitStack()
    with ctx:
        def sb(name, shape, dt=F32):
            return ctx.enter_context(nc.sbuf_tensor(name, shape, dt))

        def sem(name):
            return ctx.enter_context(nc.semaphore(name))

        x_slots = nc.dram_tensor("x_slots", (ROWS + NT * P * K, D), F32, kind="Internal").ap()
        y_slots = nc.dram_tensor("y_slots", (ROWS, D), F32, kind="Internal").ap()

        cst = sb("cst", [P, C_END])
        ident, tri, ones = cst[:, C_ID:C_ID + P], cst[:, C_TRI:C_TRI + P], cst[:, C_ONE:C_ONE + P]
        blockmask = cst[:, C_BLK:C_BLK + P]
        base_tab = cst[:, C_BASE:C_TRASH].rearrange("p (b n) -> p b n", b=B)
        trash_tab = cst[:, C_TRASH:C_IOTA].rearrange("p (b n) -> p b n", b=B)
        iota = cst[:, C_IOTA:C_END]
        gm = sb("gm", [P, S])
        wqT_s, wkT_s, wv_s, woT_s = (sb(n, [P, D]) for n in ("wqT_s", "wkT_s", "wv_s", "woT_s"))
        wvoT_s = sb("wvoT_s", [P, D])
        bq_s, bk_s, bv_s = sb("bq_s", [P, 1]), sb("bk_s", [P, 1]), sb("bv_s", [P, 1])
        bv_wide = sb("bv_wide", [P, P])
        bo_s, beff = sb("bo_s", [P, D]), sb("beff", [P, D])
        gateT_s = sb("gateT_s", [P, E])
        u1T_s, v1_s = sb("u1T_s", [RANK, D]), sb("v1_s", [RANK, DFF])
        u2T_s, v2_s = sb("u2T_s", [RANK, DFF]), sb("v2_s", [RANK, D])
        f1_s, f2_s = sb("f1_s", [P, DFF]), sb("f2_s", [P, FC, D])
        b1_s, b2_s = sb("b1_s", [P, FC]), sb("b2_s", [P, D])
        zeros = sb("zeros", [P, 2560])
        mhalf = sb("mhalf", [P, T])

        xT_s, xn_s, xb_s = sb("xT_s", [P, S]), sb("xn_s", [P, T, D]), sb("xb_s", [P, T, D])
        QT, KT, V = sb("QT", [P, S]), sb("KT", [P, S]), sb("V", [P, T, D])
        prob = sb("prob", [P, 2, S])
        PT = sb("PT", [P, T, P])
        nmax, rsum, rinv = sb("nmax", [P, T]), sb("rsum", [P, T]), sb("rinv", [P, T])
        h1 = sb("h1", [P, T, D])
        st1, mv1 = sb("st1", [P, T, 6]), sb("mv1", [P, T, 2])
        ve1, rs1 = sb("ve1", [P, T]), sb("rs1", [P, T])
        x1b = sb("x1b", [P, T, D])
        x1_all = sb("x1_all", [P, NT, D])
        x1T = sb("x1T", [P, S])
        lg, lmx, lsh, lex = sb("lg", [P, T, E]), sb("lmx", [P, T]), sb("lsh", [P, T, E]), sb("lex", [P, T, E])
        lsum, linv, pr = sb("lsum", [P, T]), sb("linv", [P, T]), sb("pr", [P, T, E])
        top, tix = sb("top", [P, T, E]), sb("tix", [P, T, E], U32)
        tixf = sb("tixf", [P, K, T])
        oh = sb("oh", [P, K, T, E])
        both = sb("both", [P, T, E])
        before = sb("before", [P, T, E])
        cnt = sb("cnt", [P, T, E])
        ohc = sb("ohc", [P, K, T, E])
        pos, fits, slot = sb("pos", [P, K, T]), sb("fits", [P, K, T]), sb("slot", [P, K, T])
        row_g, row_d = sb("row_g", [P, K * T]), sb("row_d", [P, K * T])
        row_s = sb("row_s", [P, K * T])
        sidx = sb("sidx", [P, K * T], U32)
        gidx = sb("gidx", [P, B, K * T], U32)
        wts = sb("wts", [P, B, K * T])
        Xn = sb("Xn", [P, 2, Q * D])
        XT = sb("XT", [P, 2, SLOTS])
        w13_s = sb("w13_s", [P, 2, 2 * F])
        w2_s = sb("w2_s", [P, 2, 4, D])
        sil = sb("sil", [P, 2, HALF])
        G = sb("G", [P, 2, 4, SLOTS])
        Ys = sb("Ys", [P, 2, Q * D])
        gi_s, wt_s = sb("gi_s", [P, B * K], U32), sb("wt_s", [P, B * K])
        GA = sb("GA", [P, B * K, D])
        h2 = sb("h2", [P, 2, B, D])
        x2 = sb("x2", [P, B, D])
        st2, mv2, ve2, rs2 = sb("st2", [P, B, 6]), sb("mv2", [P, B, 2]), sb("ve2", [P, B]), sb("rs2", [P, B])
        x2T = sb("x2T", [P, NJ, B * SUB])
        xv = sb("xv", [P, NJ, D])
        sm = sb("sm", [P, NJ, P])
        nm3, sum3, inv3 = sb("nm3", [P, NJ]), sb("sum3", [P, NJ]), sb("inv3", [P, NJ])
        p3, p3T = sb("p3", [P, NJ, P]), sb("p3T", [P, NJ, P])
        h3 = sb("h3", [P, NJ, D])
        st3, mv3, ve3, rs3 = sb("st3", [P, NJ, 6]), sb("mv3", [P, NJ, 2]), sb("ve3", [P, NJ]), sb("rs3", [P, NJ])
        x3, x3b = sb("x3", [P, NJ, D]), sb("x3b", [P, NJ, D])
        x3T = sb("x3T", [P, NJ * P])
        H = sb("H", [P, FC, NJ * P])
        h4 = sb("h4", [P, NJ, D])
        st4, mv4, ve4, rs4 = sb("st4", [P, NJ, 6]), sb("mv4", [P, NJ, 2]), sb("ve4", [P, NJ]), sb("rs4", [P, NJ])
        x4 = sb("x4", [P, NJ, D])

        PS = ctx.enter_context(nc.psum_tensor("PS", [P, 8, 512], F32))

        s_ld0 = sem("s_ld0")
        s_ld1 = sem("s_ld1")
        s_xT = sem("s_xT")
        s_xn = sem("s_xn")
        s_zero = sem("s_zero")
        s_x1all = sem("s_x1all")
        s_Xn = [sem("s_Xn0"), sem("s_Xn1")]
        s_w = [sem("s_w0"), sem("s_w1")]
        s_yst = [sem("s_yst0"), sem("s_yst1")]
        s_out = sem("s_out")
        s_init = sem("s_init")
        s_xb = sem("s_xb")
        s_rs1 = sem("s_rs1")
        s_sc = sem("s_sc")
        s_pool = sem("s_pool")
        s_ga = sem("s_ga")
        s_rs2, s_rs3, s_rs4 = sem("s_rs2"), sem("s_rs3"), sem("s_rs4")
        s_prep_mm = sem("s_prep_mm")
        s_prep_ev = sem("s_prep_ev")
        s_bvw = sem("s_bvw")
        s_k_mm, s_q_mm, s_v_mm = sem("s_k_mm"), sem("s_q_mm"), sem("s_v_mm")
        s_k_ev, s_q_ev = sem("s_k_ev"), sem("s_q_ev")
        s_v0_ev, s_v1_ev = sem("s_v0_ev"), sem("s_v1_ev")
        s_s = sem("s_s")
        s_max = sem("s_max")
        s_exp = sem("s_exp")
        s_t = sem("s_t")
        s_e0, s_e1 = sem("s_e0"), sem("s_e1")
        s_pv = sem("s_pv")
        s_o = sem("s_o")
        s_own = sem("s_own")
        s_var1 = sem("s_var1")
        s_x1 = sem("s_x1")
        s_r_mm = sem("s_r_mm")
        s_r_ev = sem("s_r_ev")
        s_lsh = sem("s_lsh")
        s_lex = sem("s_lex")
        s_both = sem("s_both")
        s_idx = sem("s_idx")
        s_XT_mm, s_XT_ev = sem("s_XT_mm"), sem("s_XT_ev")
        s_h = sem("s_h")
        s_sil = sem("s_sil")
        s_g = sem("s_g")
        s_y = sem("s_y")
        s_ye = sem("s_ye")
        s_comb = sem("s_comb")
        s_var2, s_var3, s_var4 = sem("s_var2"), sem("s_var3"), sem("s_var4")
        s_x2 = sem("s_x2")
        s_x2T_mm, s_x2T_ev = sem("s_x2T_mm"), sem("s_x2T_ev")
        s_xv_mm, s_xv_ev = sem("s_xv_mm"), sem("s_xv_ev")
        s_s3 = sem("s_s3")
        s_sm = sem("s_sm")
        s_p3 = sem("s_p3")
        s_p3T_mm, s_p3T_ev = sem("s_p3T_mm"), sem("s_p3T_ev")
        s_pv3 = sem("s_pv3")
        s_h3 = sem("s_h3")
        s_x3 = sem("s_x3")
        s_x3T_mm, s_x3T_ev = sem("s_x3T_mm"), sem("s_x3T_ev")
        s_f1 = sem("s_f1")
        s_gelu = sem("s_gelu")
        s_f2 = sem("s_f2")
        s_h4 = sem("s_h4")
        s_x4 = sem("s_x4")

        block = ctx.enter_context(nc.Block())

        @block.sync
        def _(sp):
            def load(dst, src, s):
                sp.dma_start(dst, src).then_inc(s, 16)

            load(wkT_s[:, :], wkT, s_ld0)
            load(xT_s[:, :], xT[:, 0:S], s_xT)
            load(wqT_s[:, :], wqT, s_ld0)
            load(wv_s[:, :], wv, s_ld0)
            load(woT_s[:, :], woT, s_ld0)
            load(gm[:, :], gmask, s_ld0)
            load(cst[:, :], consts, s_ld0)
            load(bq_s[:, :], bq, s_ld0)
            load(bk_s[:, :], bk, s_ld0)
            load(bv_s[:, :], bv, s_ld0)
            load(bo_s[:, :], bo, s_ld0)
            load(gateT_s[:, :], gateT, s_ld0)
            load(b1_s[:, :], b1, s_ld0)
            load(b2_s[:, :], b2, s_ld0)
            load(xn_s[:, :, :], x[0:S, :].rearrange("(t p) d -> p t d", p=P), s_xn)
            load(u1T_s[:, :], u1T, s_ld1)
            load(v1_s[:, :], v1, s_ld1)
            load(u2T_s[:, :], u2T, s_ld1)
            load(v2_s[:, :], v2, s_ld1)
            sp.wait_ge(s_init, 1)
            zr = x_slots[0:ROWS, :].rearrange("(q p t) d -> q p (t d)", p=P, t=2560 // D)
            for q in range(zr.shape[0]):
                load(zr[q], zeros[:, :], s_zero)

            def weights(j, u):
                load(w13_s[:, u, :], w13[bass.ds(j % E, 1), :, :].rearrange("e p n -> p (e n)"), s_w[u])
                load(w2_s[:, u, 0:3, :], w2[bass.ds(j % E, 1), 0:3 * P, :].rearrange("e (c p) d -> p (e c) d", p=P), s_w[u])
                load(w2_s[0:FT, u, 3, :], w2[bass.ds(j % E, 1), 3 * P:F, :].rearrange("e p d -> p (e d)"), s_w[u])

            with sp.Fori(0, B - 1) as b:
                sp.wait_ge(s_v_mm, 2 * b + 2)
                load(xT_s[:, :], xT[:, bass.ds((b + 1) * S, S)], s_xT)
                sp.wait_ge(s_xb, b + 1)
                load(xn_s[:, :, :], x[bass.ds((b + 1) * S, S), :].rearrange("(t p) d -> p t d", p=P), s_xn)
                sp.wait_ge(s_x1, b + 1)
                load(x1_all[:, bass.ds(b * T, T), :], x1b[:, :, :], s_x1all)
            weights(0, 0)
            weights(1, 1)
            sp.wait_ge(s_x1, B)
            load(x1_all[:, (B - 1) * T:NT, :], x1b[:, :, :], s_x1all)

            def slots_in(j, u):
                load(Xn[:, u, :], x_slots[bass.ds(j * SLOTS, SLOTS), :].rearrange("(p t) d -> p (t d)", p=P), s_Xn[u])

            def slots_out(j, u):
                sp.wait_ge(s_ye, j + 1)
                load(y_slots[bass.ds(j * SLOTS, SLOTS), :].rearrange("(p t) d -> p (t d)", p=P), Ys[:, u, :], s_yst[u])

            slots_in(0, 0)
            slots_in(1, 1)
            with sp.Fori(0, J // 2 - 1) as i:
                for u in range(2):
                    j = 2 * i + u
                    sp.wait_ge(s_y, j + 1)
                    weights(j + 2, u)
                    if u == 0:
                        sp.wait_ge(s_sc, 16 * K * T * (B - 1 + (i + 1) // (J // 4)))
                    slots_in(j + 2, u)
                    slots_out(j, u)
            slots_out(J - 2, 0)
            slots_out(J - 1, 1)

            def output(g):
                sp.wait_ge(s_x4, g + 1)
                for b in range(B):
                    load(out[b, bass.ds(g * P, P), :].rearrange("(j s) d -> s j d", s=SUB),
                         x4[b * SUB:(b + 1) * SUB, :, :], s_out)

            with sp.Fori(0, T) as g:
                output(g)
            sp.wait_ge(s_out, 16 * B * T)

        @block.gpsimd
        def _(pool):
            own = Steps(pool, s_pool)
            pool.memset(zeros[:, :], 0.0).then_inc(s_init, 1)
            pool.memset(mhalf[:, :], -0.5).then_inc(s_init, 1)

            def x_plus_bias(b):
                if not isinstance(b, int) or b > 0:
                    pool.wait_ge(s_o, T * b)
                else:
                    pool.wait_ge(s_prep_ev, 2)
                pool.wait_ge(s_xn, 16 * b + 16)
                pool.tensor_tensor(xb_s[:, :, :], xn_s[:, :, :], beff[:, None, :].to_broadcast([P, T, D]),
                                   ALU.add).then_inc(s_xb, 1)

            def scatter(r):
                pool.wait_ge(s_zero, 16 * (ROWS * D // (P * 2560)))
                pool.wait_ge(s_idx, r + 1)
                pool.engine_nop()
                for k in range(K):
                    for t in range(T):
                        pool.indirect_dma_start(x_slots[:, :], bass.IndirectOffsetOnAxis(ap=sidx[:, k * T + t:k * T + t + 1], axis=0),
                                                x1b[:, t, :], None).then_inc(s_sc, 16)

            def rstd1(b):
                pool.wait_ge(s_var1, b + 1)
                pool.tensor_tensor(rs1[:, :], ve1[:, :], mhalf[:, :], ALU.pow).then_inc(s_rs1, 1)

            pool.wait_ge(s_init, 2)
            x_plus_bias(0)
            rstd1(0)
            with pool.Fori(1, B) as b:
                x_plus_bias(b)
                scatter(b - 1)
                rstd1(b)
            scatter(B - 1)

            def gather(g):
                own.add(pool.tensor_copy(gi_s[:, :], gidx[:, :, :].rearrange("p b (k t) -> p (b k) t", k=K)[:, :, g]))
                own.add(pool.tensor_copy(wt_s[:, :], wts[:, :, :].rearrange("p b (k t) -> p (b k) t", k=K)[:, :, g]))
                own.close()
                for n in range(B * K):
                    pool.indirect_dma_start(GA[:, n, :], None, y_slots[:, :],
                                            bass.IndirectOffsetOnAxis(ap=gi_s[:, n:n + 1], axis=0)).then_inc(s_ga, 16)

            def rstd(n, var, s_var, r, s_rs):
                pool.wait_ge(s_var, n + 1)
                pool.tensor_tensor(r[:, :], var[:, :], mhalf[:, 0:NJ], ALU.pow).then_inc(s_rs, 1)

            for u in range(2):
                pool.wait_ge(s_yst[u], 16 * (J // 2))
            gather(0)
            rstd(0, ve2, s_var2, rs2, s_rs2)
            pool.wait_ge(s_comb, 1)
            gather(1)
            rstd(0, ve3, s_var3, rs3, s_rs3)
            with pool.Fori(1, T - 1) as g:
                rstd(g, ve2, s_var2, rs2, s_rs2)
                pool.wait_ge(s_comb, g + 1)
                gather(g + 1)
                rstd(g - 1, ve4, s_var4, rs4, s_rs4)
                rstd(g, ve3, s_var3, rs3, s_rs3)
            rstd(T - 1, ve2, s_var2, rs2, s_rs2)
            rstd(T - 2, ve4, s_var4, rs4, s_rs4)
            rstd(T - 1, ve3, s_var3, rs3, s_rs3)
            rstd(T - 1, ve4, s_var4, rs4, s_rs4)

        @block.scalar
        def _(act):
            def exps(g, t):
                act.wait_ge(s_max, g + 1)
                act.activation(prob[:, t % 2, :].rearrange("p (h n) -> p h n", h=2), PS[:, 2 * (t % 2):2 * (t % 2) + 2, :], ACT.Exp,
                               bias=nmax[:, t:t + 1], accum_out=rsum[:, t:t + 1]).then_inc(s_exp, 1)

            def q_out(b):
                act.wait_ge(s_q_mm, b + 1)
                act.activation(QT[:, :].rearrange("p (h n) -> p h n", h=2), PS[:, 2:4, :], ACT.Identity, bias=bq_s[:, 0:1]).then_inc(s_q_ev, 1)

            def v_out(b):
                act.wait_ge(s_v_mm, 2 * b + 1)
                act.activation(V[:, 0:4, :], PS[:, 4, :].rearrange("p (t d) -> p t d", t=4), ACT.Copy).then_inc(s_v0_ev, 1)

            def router_out(r, n, dst, cols, bank=7):
                act.wait_ge(s_r_mm, 4 * r + n + 1)
                act.activation(dst, PS[:, bank, 0:cols], ACT.Copy).then_inc(s_r_ev, 1)

            def router_exp(r):
                act.wait_ge(s_lsh, r + 1)
                act.activation(lex[:, :, :], lsh[:, :, :], ACT.Exp).then_inc(s_lex, 1)

            def body(b, first=False, last=False):
                for t in range(T):
                    g = b * T + t
                    act.wait_ge(s_t, 2 * g + 1)
                    act.activation(PT[:, 0:4, :], PS[:, 4, :].rearrange("p (k n) -> p k n", k=4), ACT.Copy).then_inc(s_e0, 1)
                    if t == 1 and not first:
                        router_out(b - 1, 1, x1T[:, 512:1024], 512)
                    if t + 2 < T:
                        exps(g + 2, t + 2)
                    if t == 0 and not first:
                        router_out(b - 1, 0, x1T[:, 0:512], 512)
                    if t == 1 and not first:
                        router_out(b - 1, 2, lg[:, :, :].rearrange("p t e -> p (t e)"), T * E)
                    if t == 2 and not first:
                        router_exp(b - 1)
                    if t == 4 and not first:
                        router_out(b - 1, 3, cnt[:, :, :].rearrange("p t e -> p (t e)"), T * E)
                if not last:
                    q_out(b + 1)
                    v_out(b + 1)
                    exps(b * T + T, 0)
                    exps(b * T + T + 1, 1)

            act.wait_ge(s_ld0, 16 * 13)
            q_out(0)
            v_out(0)
            exps(0, 0)
            exps(1, 1)
            body(0, first=True)
            with act.Fori(1, B - 1) as b:
                body(b)
            body(B - 1, last=True)

            router_out(B - 1, 0, x1T[:, 0:512], 512)
            router_out(B - 1, 1, x1T[:, 512:1024], 512)
            router_out(B - 1, 2, lg[:, :, :].rearrange("p t e -> p (t e)"), T * E)
            router_exp(B - 1)

            def slots_T(j, u):
                act.wait_ge(s_XT_mm, j + 1)
                act.activation(XT[:, u, 0:512], PS[:, 0, :], ACT.Copy)
                act.activation(XT[:, u, 512:SLOTS], PS[:, 1, 0:SLOTS - 512], ACT.Copy).then_inc(s_XT_ev, 1)

            def silu(j, k):
                act.wait_ge(s_h, NU * j + k + 1)
                n = P if k < 6 else FT
                act.activation(sil[0:n, k % 2, :], PS[0:n, 2 + 2 * (k % 2), 0:HALF], ACT.Silu).then_inc(s_sil, 1)

            def pass_(j, u, last=False):
                for k in range(2, NU):
                    silu(j, k)
                if not last:
                    slots_T(j + 1, 1 - u)
                    silu(j + 1, 0)
                    silu(j + 1, 1)

            slots_T(0, 0)
            silu(0, 0)
            silu(0, 1)
            pass_(0, 0)
            pass_(1, 1)
            router_out(B - 1, 3, cnt[:, :, :].rearrange("p t e -> p (t e)"), T * E, bank=1)
            with act.Fori(1, J // 2 - 1) as i:
                pass_(2 * i, 0)
                pass_(2 * i + 1, 1)
            pass_(J - 2, 0)
            pass_(J - 1, 1, last=True)

            def gelu(g, c):
                act.wait_ge(s_f1, FC * g + c + 1)
                act.activation(H[:, c, :], PS[:, 5 + c % 2, :], ACT.Gelu_apprx_tanh, bias=b1_s[:, c:c + 1]).then_inc(s_gelu, 1)

            def copy_out(mm, n, dst, bank, ev):
                act.wait_ge(mm, n)
                act.activation(dst, PS[:, bank, :].rearrange("p (k n) -> p k n", k=4), ACT.Copy).then_inc(ev, 1)

            def group(g, first=False):
                act.wait_ge(s_x2T_mm, g + 1)
                act.activation(x2T[:, :, :].rearrange("p j (b s) -> p b j s", b=B), PS[:, 0, :].rearrange("p (b j s) -> p b j s", b=B, j=NJ),
                               ACT.Copy).then_inc(s_x2T_ev, 1)
                if not first:
                    gelu(g - 1, 0)
                    gelu(g - 1, 1)
                copy_out(s_xv_mm, g + 1, xv[:, :, :], 1, s_xv_ev)
                act.wait_ge(s_sm, 2 * g + 2)
                for j in range(NJ):
                    act.activation(p3[:, j, :], sm[:, j, :], ACT.Exp, bias=nm3[:, j:j + 1],
                                   accum_out=sum3[:, j:j + 1]).then_inc(s_p3, 1)
                if not first:
                    gelu(g - 1, 2)
                    gelu(g - 1, 3)
                copy_out(s_p3T_mm, g + 1, p3T[:, :, :], 3, s_p3T_ev)
                copy_out(s_x3T_mm, g + 1, x3T[:, :].rearrange("p (k n) -> p k n", k=4), 0, s_x3T_ev)

            group(0, first=True)
            with act.Fori(1, T) as g:
                group(g)
            for c in range(FC):
                gelu(T - 1, c)

        @block.vector
        def _(dve):
            own = Steps(dve, s_own)

            def k_out(b):
                dve.wait_ge(s_k_mm, b + 1)
                dve.scalar_tensor_tensor(out=KT[:, :].rearrange("p (h n) -> p h n", h=2), in0=PS[:, 0:2, :],
                                         scalar=bk_s[:, 0:1], in1=gm[:, :].rearrange("p (h n) -> p h n", h=2),
                                         op0=ALU.add, op1=ALU.mult).then_inc(s_k_ev, 1)

            def v_out(b):
                dve.wait_ge(s_v_mm, 2 * b + 2)
                dve.tensor_copy(V[:, 4:8, :], PS[:, 5, :].rearrange("p (t d) -> p t d", t=4)).then_inc(s_v1_ev, 1)

            def row_max(g, t):
                dve.wait_ge(s_s, g + 1)
                dve.tensor_reduce(nmax[:, t:t + 1], PS[:, 2 * (t % 2):2 * (t % 2) + 2, :], AX.XY, ALU.max, negate=True).then_inc(s_max, 1)

            def residual(g, t):
                dve.wait_ge(s_exp, g + 1)
                own.add(dve.reciprocal(rinv[:, t:t + 1], rsum[:, t:t + 1]))
                dve.wait_ge(s_pv, g + 1)
                own.wait()
                dve.scalar_tensor_tensor(out=h1[:, t, :], in0=PS[:, 6, 0:D], scalar=rinv[:, t:t + 1],
                                         in1=xb_s[:, t, :], op0=ALU.mult, op1=ALU.add).then_inc(s_o, 1)
                dve.wait_ge(s_o, g + 1)
                own.add(dve.bn_stats(st1[:, t, :], h1[:, t, :]))
                own.wait()
                own.add(dve.bn_aggr(mv1[:, t, :], st1[:, t, :]))

            def var1(b):
                own.wait()
                dve.tensor_scalar(ve1[:, :], mv1[:, :, 1], EPS, None, ALU.add).then_inc(s_var1, 1)

            def ln1(b, first=False):
                dve.wait_ge(s_rs1, b + 1)
                if not first:
                    dve.wait_ge(s_sc, 16 * K * T * b)
                    dve.wait_ge(s_x1all, 16 * b)
                for t in range(T):
                    ins = dve.tensor_scalar(x1b[:, t, :], h1[:, t, :], mv1[:, t, 0:1], rs1[:, t:t + 1], ALU.subtract, ALU.mult)
                ins.then_inc(s_x1, 1)

            def router_shift(r):
                dve.wait_ge(s_r_ev, 4 * r + 3)
                own.add(dve.tensor_reduce(lmx[:, :], lg[:, :, :], AX.X, ALU.max))
                own.wait()
                dve.tensor_tensor(lsh[:, :, :], lg[:, :, :], lmx[:, :, None].to_broadcast([P, T, E]), ALU.subtract).then_inc(s_lsh, 1)

            def router_top(r):
                dve.wait_ge(s_lex, r + 1)
                own.add(dve.tensor_reduce(lsum[:, :], lex[:, :, :], AX.X, ALU.add))
                own.wait()
                own.add(dve.reciprocal(linv[:, :], lsum[:, :]))
                own.wait()
                own.add(dve.tensor_tensor(pr[:, :, :], lex[:, :, :], linv[:, :, None].to_broadcast([P, T, E]), ALU.mult))
                own.wait()
                for t in range(T):
                    own.add(dve.max(top[:, t, :], pr[:, t, :]))
                for t in range(T):
                    own.wait(back=T - 1)
                    own.add(dve.max_index(tix[:, t, :], top[:, t, :], pr[:, t, :]))
                own.wait()
                own.add(dve.tensor_copy(tixf[:, :, :], tix[:, :, 0:K].rearrange("p t k -> p k t")))

            def router_choice(r):
                own.wait()
                own.add(dve.tensor_tensor(oh[:, :, :, :].rearrange("p k t e -> p (k t) e"),
                                          tixf[:, :, :].rearrange("p k t -> p (k t)")[:, :, None].to_broadcast([P, K * T, E]),
                                          iota[:, None, :].to_broadcast([P, K * T, E]), ALU.is_equal))
                own.wait()
                own.add(dve.tensor_tensor(both[:, :, :], oh[:, 0, :, :], oh[:, 1, :, :], ALU.add))
                own.add(dve.memset(before[:, 0, :], 0.0))
                for t in range(1, T):
                    own.wait()
                    ins = dve.tensor_tensor(before[:, t, :], before[:, t - 1, :], both[:, t - 1, :], ALU.add)
                    if t < T - 1:
                        own.add(ins)
                ins.then_inc(s_both, 1)

            def router_rows(r):
                dve.wait_ge(s_r_ev, 4 * r + 4)
                own.add(dve.tensor_tensor(ohc[:, :, :, :], oh[:, :, :, :], cnt[:, None, :, :].to_broadcast([P, K, T, E]), ALU.mult))
                own.wait()
                own.add(dve.tensor_reduce(pos[:, :, :].rearrange("p k t -> p (k t)"), ohc[:, :, :, :].rearrange("p k t e -> p (k t) e"), AX.X, ALU.add))
                own.wait()
                own.add(dve.tensor_scalar(fits[:, :, :], pos[:, :, :], float(CAP), None, ALU.is_le))
                own.add(dve.tensor_scalar(slot[:, :, :], pos[:, :, :], float(CAP), None, ALU.min))
                own.wait()
                own.add(dve.scalar_tensor_tensor(out=row_d[:, :], in0=tixf[:, :, :].rearrange("p k t -> p (k t)"), scalar=float(SLOTS),
                                                 in1=slot[:, :, :].rearrange("p k t -> p (k t)"), op0=ALU.mult, op1=ALU.add))
                own.wait()
                own.add(dve.tensor_tensor(row_g[:, :], row_d[:, :], base_tab[:, r, :], ALU.add))
                own.wait()
                own.add(dve.tensor_tensor(row_d[:, :], row_g[:, :], trash_tab[:, r, :], ALU.subtract))
                own.wait()
                own.add(dve.tensor_tensor(row_s[:, :], row_d[:, :], fits[:, :, :].rearrange("p k t -> p (k t)"), ALU.mult))
                own.wait()
                own.add(dve.tensor_tensor(row_d[:, :], row_s[:, :], trash_tab[:, r, :], ALU.add))
                own.wait()
                dve.tensor_copy(gidx[:, r, :], row_g[:, :])
                dve.tensor_tensor(wts[:, r, :].rearrange("p (k t) -> p k t", k=K), top[:, :, 0:K].rearrange("p t k -> p k t"),
                                  fits[:, :, :], ALU.mult)
                dve.tensor_copy(sidx[:, :], row_d[:, :]).then_inc(s_idx, 1)

            def body(b, first=False, last=False):
                for t in range(T):
                    g = b * T + t
                    dve.wait_ge(s_t, 2 * g + 2)
                    dve.tensor_copy(PT[:, 4:8, :], PS[:, 5, :].rearrange("p (k n) -> p k n", k=4)).then_inc(s_e1, 1)
                    if t == 2 and not first:
                        router_shift(b - 1)
                    if t + 2 < T:
                        row_max(g + 2, t + 2)
                    if t == 0:
                        dve.wait_ge(s_xb, b + 1)
                    residual(g, t)
                    if t == 2 and not first:
                        router_top(b - 1)
                    if t == 3 and not first:
                        router_choice(b - 1)
                    if t == 4 and not first:
                        router_rows(b - 1)
                    if t == 6 and not last:
                        k_out(b + 1)
                var1(b)
                if not last:
                    v_out(b + 1)
                    row_max(b * T + T, 0)
                    row_max(b * T + T + 1, 1)
                ln1(b, first)
                own.close()

            dve.wait_ge(s_ld0, 16 * 13)
            dve.tensor_copy(bv_wide[:, :], bv_s[:, 0:1].to_broadcast([P, P])).then_inc(s_bvw, 1)
            k_out(0)
            dve.wait_ge(s_prep_mm, 1)
            dve.tensor_copy(wvoT_s[:, :], PS[:, 6, 0:D]).then_inc(s_prep_ev, 1)
            dve.wait_ge(s_prep_mm, 2)
            dve.tensor_tensor(beff[:, :], PS[:, 7, 0:D], bo_s[:, :], ALU.add).then_inc(s_prep_ev, 1)
            v_out(0)
            row_max(0, 0)
            row_max(1, 1)
            dve.wait_ge(s_prep_mm, 3)
            dve.tensor_copy(f1_s[:, :], PS[:, 6, :]).then_inc(s_prep_ev, 1)
            dve.wait_ge(s_prep_mm, 4)
            dve.tensor_copy(f2_s[:, :, :], PS[:, 7, :].rearrange("p (c d) -> p c d", c=FC)).then_inc(s_prep_ev, 1)
            body(0, first=True)
            with dve.Fori(1, B - 1) as b:
                body(b)
            body(B - 1, last=True)
            router_shift(B - 1)
            router_top(B - 1)
            router_choice(B - 1)

            def gated(j, u, k):
                dve.wait_ge(s_sil, NU * j + k + 1)
                c, h = k // 2, k % 2
                if c < 3:
                    dve.tensor_tensor(G[:, u, c, h * HALF:(h + 1) * HALF], sil[:, k % 2, :], PS[:, 3 + 2 * (k % 2), 0:HALF],
                                      ALU.mult).then_inc(s_g, 1)
                else:
                    dve.tensor_tensor(G[0:FT, u, c, h * HALF:(h + 1) * HALF], sil[0:FT, k % 2, :], PS[FT:2 * FT, 2 + 2 * (k % 2), 0:HALF],
                                      ALU.mult).then_inc(s_g, 1)

            def pass_(j, u, last=False, started=True):
                for k in range(2, NU):
                    gated(j, u, k)
                if not last:
                    gated(j + 1, 1 - u, 0)
                    gated(j + 1, 1 - u, 1)
                dve.wait_ge(s_y, j + 1)
                if started:
                    dve.wait_ge(s_yst[u], 16 * (j // 2) if isinstance(j, int) else 16 * half_of(j))
                dve.tensor_copy(Ys[:, u, 0:512], PS[:, 6, :])
                dve.tensor_copy(Ys[:, u, 512:Q * D], PS[:, 7, 0:Q * D - 512]).then_inc(s_ye, 1)

            halves = {}

            def half_of(j):
                return halves["i"]

            gated(0, 0, 0)
            gated(0, 0, 1)
            pass_(0, 0, started=False)
            pass_(1, 1, started=False)
            router_rows(B - 1)
            own.close()
            with dve.Fori(1, J // 2 - 1) as i:
                halves["i"] = i
                pass_(2 * i, 0)
                pass_(2 * i + 1, 1)
            pass_(J - 2, 0)
            pass_(J - 1, 1, last=True)

            def ffn_out(g):
                dve.wait_ge(s_f2, g + 1)
                dve.tensor_tensor(h4[:, :, :], PS[:, 7, :].rearrange("p (j d) -> p j d", j=NJ), x3b[:, :, :], ALU.add).then_inc(s_h4, 1)
                dve.wait_ge(s_h4, g + 1)
                stats(h4, st4, mv4, ve4, s_var4)

            def stats(h, st, mv, ve, s_var):
                for j in range(NJ):
                    own.add(dve.bn_stats(st[:, j, :], h[:, j, :]))
                for j in range(NJ):
                    own.wait(back=NJ - 1)
                    own.add(dve.bn_aggr(mv[:, j, :], st[:, j, :]))
                own.wait()
                dve.tensor_scalar(ve[:, :], mv[:, :, 1], EPS, None, ALU.add).then_inc(s_var, 1)

            def normal(h, mv, rs, xo, s_x):
                for j in range(NJ):
                    ins = dve.tensor_scalar(xo[:, j, :], h[:, j, :], mv[:, j, 0:1], rs[:, j:j + 1], ALU.subtract, ALU.mult)
                ins.then_inc(s_x, 1)

            def ffn_norm(g, first=False):
                dve.wait_ge(s_rs4, g + 1)
                if not first:
                    dve.wait_ge(s_out, 16 * B * g)
                normal(h4, mv4, rs4, x4, s_x4)

            def group(g, first=False, second=False):
                dve.wait_ge(s_ga, 16 * B * K * (g + 1))
                for b in range(B):
                    own.add(dve.scalar_tensor_tensor(out=h2[:, 0, b, :], in0=GA[:, b * K, :], scalar=wt_s[:, b * K:b * K + 1],
                                                     in1=x1_all[:, bass.ds(b * T + g, 1), :].rearrange("p o d -> p (o d)"), op0=ALU.mult, op1=ALU.add))
                for b in range(B):
                    own.wait(back=B - 1)
                    ins = dve.scalar_tensor_tensor(out=h2[:, 1, b, :], in0=GA[:, b * K + 1, :], scalar=wt_s[:, b * K + 1:b * K + 2],
                                                   in1=h2[:, 0, b, :], op0=ALU.mult, op1=ALU.add)
                    own.add(ins)
                own.wait()
                dve.nop().then_inc(s_comb, 1)
                stats(h2[:, 1, :, :], st2, mv2, ve2, s_var2)
                dve.wait_ge(s_rs2, g + 1)
                normal(h2[:, 1, :, :], mv2, rs2, x2, s_x2)
                dve.wait_ge(s_s3, g + 1)
                dve.scalar_tensor_tensor(out=sm[:, :, :], in0=PS[:, 2, :].rearrange("p (j n) -> p j n", j=NJ), scalar=float(D) ** -0.5,
                                         in1=blockmask[:, None, :].to_broadcast([P, NJ, P]), op0=ALU.mult, op1=ALU.add).then_inc(s_sm, 1)
                dve.wait_ge(s_sm, 2 * g + 1)
                dve.tensor_reduce(nm3[:, :], sm[:, :, :], AX.X, ALU.max, negate=True).then_inc(s_sm, 1)
                if not first:
                    ffn_out(g - 1)
                dve.wait_ge(s_p3, NJ * (g + 1))
                own.add(dve.reciprocal(inv3[:, :], sum3[:, :]))
                own.wait()
                dve.wait_ge(s_pv3, g + 1)
                for j in range(NJ):
                    own.add(dve.scalar_tensor_tensor(out=h3[:, j, :], in0=PS[:, 4, j * D:(j + 1) * D], scalar=inv3[:, j:j + 1],
                                                     in1=xv[:, j, :], op0=ALU.mult, op1=ALU.add))
                own.wait()
                dve.nop().then_inc(s_h3, 1)
                stats(h3, st3, mv3, ve3, s_var3)
                if not first:
                    ffn_norm(g - 1, second)
                dve.wait_ge(s_rs3, g + 1)
                normal(h3, mv3, rs3, x3, s_x3)
                dve.wait_ge(s_x3, 2 * g + 1)
                dve.tensor_tensor(x3b[:, :, :], x3[:, :, :], b2_s[:, None, :].to_broadcast([P, NJ, D]), ALU.add).then_inc(s_x3, 1)
                own.close()

            dve.wait_ge(s_x1all, 16 * B)
            group(0, first=True)
            group(1, second=True)
            with dve.Fori(2, T) as g:
                group(g)
            ffn_out(T - 1)
            ffn_norm(T - 1)

        @block.tensor
        def _(pe):
            def k_mm(b):
                pe.wait_ge(s_xT, 16 * (b + 1))
                for h in range(2):
                    mm = pe.matmul(PS[:, h, :], wkT_s[:, :], xT_s[:, h * 512:(h + 1) * 512], start=True, stop=True)
                mm.then_inc(s_k_mm, 1)

            def q_mm(b):
                for h in range(2):
                    mm = pe.matmul(PS[:, 2 + h, :], wqT_s[:, :], xT_s[:, h * 512:(h + 1) * 512], start=True, stop=True)
                mm.then_inc(s_q_mm, 1)

            def v_mm(b):
                for h in range(2):
                    for t in range(4):
                        mm = pe.matmul(PS[:, 4 + h, t * D:(t + 1) * D], xT_s[:, (4 * h + t) * P:(4 * h + t + 1) * P], wvoT_s[:, :],
                                       start=True, stop=True)
                    mm.then_inc(s_v_mm, 1)

            def scores(g, t):
                for h in range(2):
                    mm = pe.matmul(PS[:, 2 * (t % 2) + h, :], QT[:, t * P:(t + 1) * P], KT[:, h * 512:(h + 1) * 512], start=True, stop=True)
                mm.then_inc(s_s, 1)

            def turn(src, cols, bank, n):
                for i in range(n):
                    mm = pe.transpose(PS[:, bank, i * P:(i + 1) * P], cols(i) if src is None else src[:, i, :], ident)
                return mm

            def router_turn(r, h):
                if h == 0:
                    pe.wait_ge(s_x1, r + 1)
                if not isinstance(r, int) or r or h:
                    pe.wait_ge(s_r_ev, 4 * r + h)
                else:
                    pe.wait_ge(s_prep_ev, 4)
                for t in range(4):
                    mm = pe.transpose(PS[:, 7, t * P:(t + 1) * P], x1b[:, 4 * h + t, :], ident)
                mm.then_inc(s_r_mm, 1)

            def router_logits(r):
                pe.wait_ge(s_r_ev, 4 * r + 2)
                for t in range(T):
                    mm = pe.matmul(PS[:, 7, t * E:(t + 1) * E], x1T[:, t * P:(t + 1) * P], gateT_s[:, :], start=True, stop=True)
                mm.then_inc(s_r_mm, 1)

            def router_count(r, bank=7):
                pe.wait_ge(s_both, r + 1)
                pe.matmul(PS[:, bank, 0:T * E], tri, both[:, :, :].rearrange("p t e -> p (t e)"), start=True, stop=False)
                pe.matmul(PS[:, bank, 0:T * E], ones, before[:, :, :].rearrange("p t e -> p (t e)"), start=False, stop=True).then_inc(s_r_mm, 1)

            def body(b, first=False, last=False):
                for t in range(T):
                    g = b * T + t
                    pe.wait_ge(s_exp, g + 1)
                    for h, ev in ((0, s_e0), (1, s_e1)):
                        if not (first and t == 0):
                            pe.wait_ge(ev, g)
                        if t == 0:
                            pe.wait_ge((s_v0_ev, s_v1_ev)[h], b + 1)
                        for k in range(4):
                            mm = pe.transpose(PS[:, 4 + h, k * P:(k + 1) * P], prob[:, t % 2, (4 * h + k) * P:(4 * h + k + 1) * P], ident)
                        mm.then_inc(s_t, 1)
                    if t == 1 and not first:
                        router_turn(b - 1, 1)
                    if t == 7 and not last:
                        q_mm(b + 1)
                    if t + 2 < T:
                        scores(g + 2, t + 2)
                    if t == 4 and not first:
                        router_count(b - 1)
                    pe.wait_ge(s_e0, g + 1)
                    pe.wait_ge(s_e1, g + 1)
                    if not (first and t == 0):
                        pe.wait_ge(s_o, g)
                    for k in range(T):
                        mm = pe.matmul(PS[:, 6, 0:D], PT[:, k, :], V[:, k, :], start=(k == 0), stop=(k == T - 1))
                    mm.then_inc(s_pv, 1)
                    if t == 0 and not first:
                        router_turn(b - 1, 0)
                    if t == 1 and not first:
                        router_logits(b - 1)
                    if t == 6 and not last:
                        k_mm(b + 1)
                if not last:
                    v_mm(b + 1)
                    pe.wait_ge(s_k_ev, b + 2)
                    pe.wait_ge(s_q_ev, b + 2)
                    scores(b * T + T, 0)
                    scores(b * T + T + 1, 1)

            pe.wait_ge(s_ld0, 16 * 13)
            k_mm(0)
            q_mm(0)
            pe.matmul(PS[:, 6, 0:D], wv_s[:, :], woT_s[:, :], start=True, stop=True).then_inc(s_prep_mm, 1)
            pe.wait_ge(s_bvw, 1)
            pe.matmul(PS[:, 7, 0:D], bv_wide[:, :], woT_s[:, :], start=True, stop=True).then_inc(s_prep_mm, 1)
            pe.wait_ge(s_prep_ev, 1)
            v_mm(0)
            pe.wait_ge(s_k_ev, 1)
            pe.wait_ge(s_q_ev, 1)
            scores(0, 0)
            scores(1, 1)
            pe.wait_ge(s_ld1, 64)
            pe.wait_ge(s_prep_ev, 2)
            pe.matmul(PS[:, 6, :], u1T_s[:, :], v1_s[:, :], start=True, stop=True).then_inc(s_prep_mm, 1)
            for c in range(FC):
                mm = pe.matmul(PS[:, 7, c * D:(c + 1) * D], u2T_s[:, c * P:(c + 1) * P], v2_s[:, :], start=True, stop=True)
            mm.then_inc(s_prep_mm, 1)
            pe.wait_ge(s_prep_ev, 4)
            body(0, first=True)
            with pe.Fori(1, B - 1) as b:
                body(b)
            body(B - 1, last=True)
            router_turn(B - 1, 0)
            router_turn(B - 1, 1)
            router_logits(B - 1)

            def slots_T(j, u, n):
                pe.wait_ge(s_Xn[u], 16 * (n + 1))
                for q in range(Q):
                    mm = pe.transpose(PS[:, q // 4, (q % 4) * P:(q % 4 + 1) * P], Xn[:, u, q * D:(q + 1) * D], ident)
                mm.then_inc(s_XT_mm, 1)

            def unit(j, u, k, n, first=False):
                if k == 0:
                    pe.wait_ge(s_XT_ev, j + 1)
                    pe.wait_ge(s_w[u], 48 * (n + 1))
                if not first:
                    pe.wait_ge(s_g, NU * j + k - 1)
                c, h = k // 2, k % 2
                rhs = XT[:, u, h * HALF:(h + 1) * HALF]
                bank = 2 + 2 * (k % 2)
                mm = pe.matmul(PS[:, bank, 0:HALF], w13_s[:, u, c * P:(c + 1) * P], rhs, start=True, stop=True)
                if c < 3:
                    mm = pe.matmul(PS[:, bank + 1, 0:HALF], w13_s[:, u, (4 + c) * P:(5 + c) * P], rhs, start=True, stop=True)
                mm.then_inc(s_h, 1)

            def down(j, u, first=False):
                pe.wait_ge(s_g, NU * (j + 1))
                if not first:
                    pe.wait_ge(s_ye, j)
                for q in range(Q):
                    for c in range(4):
                        n = P if c < 3 else FT
                        mm = pe.matmul(PS[:, 6 + q // 4, (q % 4) * D:(q % 4 + 1) * D], G[0:n, u, c, q * P:(q + 1) * P], w2_s[0:n, u, c, :],
                                       start=(c == 0), stop=(c == 3))
                mm.then_inc(s_y, 1)

            def pass_(j, u, n, first=False, last=False):
                for k in range(2, NU):
                    unit(j, u, k, n)
                if not last:
                    m = n + (1 if u else 0)
                    slots_T(j + 1, 1 - u, m)
                    unit(j + 1, 1 - u, 0, m)
                    unit(j + 1, 1 - u, 1, m)
                down(j, u, first)

            slots_T(0, 0, 0)
            unit(0, 0, 0, 0, first=True)
            unit(0, 0, 1, 0, first=True)
            pass_(0, 0, 0, first=True)
            pass_(1, 1, 0)
            router_count(B - 1, bank=1)
            pe.wait_ge(s_r_ev, 4 * B)
            with pe.Fori(1, J // 2 - 1) as i:
                pass_(2 * i, 0, i)
                pass_(2 * i + 1, 1, i)
            pass_(J - 2, 0, J // 2 - 1)
            pass_(J - 1, 1, J // 2 - 1, last=True)

            def ffn_up(g, c):
                if c == 0:
                    pe.wait_ge(s_x3T_ev, g + 1)
                if c >= 2:
                    pe.wait_ge(s_gelu, FC * g + c - 1)
                pe.matmul(PS[:, 5 + c % 2, :], f1_s[:, c * P:(c + 1) * P], x3T[:, :], start=True, stop=True).then_inc(s_f1, 1)

            def ffn_down(g, tiles, first=False):
                pe.wait_ge(s_gelu, FC * g + FC)
                if tiles[0] == 0 and not first:
                    pe.wait_ge(s_h4, g)
                for j in tiles:
                    for c in range(FC):
                        mm = pe.matmul(PS[:, 7, j * D:(j + 1) * D], H[:, c, j * P:(j + 1) * P], f2_s[:, c, :], start=(c == 0), stop=(c == FC - 1))
                if tiles[-1] == NJ - 1:
                    mm.then_inc(s_f2, 1)

            def cols(j):
                return x2T[:, j, :]

            def group(g, first=False, second=False):
                pe.wait_ge(s_x2, g + 1)
                if not first:
                    pe.wait_ge(s_x3T_ev, g)
                for b in range(B):
                    mm = pe.transpose(PS[:, 0, b * P:(b + 1) * P], x2[:, b, :], ident)
                mm.then_inc(s_x2T_mm, 1)
                if not first:
                    ffn_up(g - 1, 0)
                    ffn_up(g - 1, 1)
                pe.wait_ge(s_x2T_ev, g + 1)
                for j in range(NJ):
                    mm = pe.transpose(PS[:, 1, j * P:(j + 1) * P], cols(j), ident)
                mm.then_inc(s_xv_mm, 1)
                for j in range(NJ):
                    mm = pe.matmul(PS[:, 2, j * P:(j + 1) * P], cols(j), cols(j), start=True, stop=True)
                mm.then_inc(s_s3, 1)
                if not first:
                    ffn_up(g - 1, 2)
                    ffn_up(g - 1, 3)
                pe.wait_ge(s_p3, NJ * (g + 1))
                for j in range(NJ):
                    mm = pe.transpose(PS[:, 3, j * P:(j + 1) * P], p3[:, j, :], ident)
                mm.then_inc(s_p3T_mm, 1)
                if not first:
                    ffn_down(g - 1, [0, 1], second)
                pe.wait_ge(s_p3T_ev, g + 1)
                pe.wait_ge(s_xv_ev, g + 1)
                for j in range(NJ):
                    mm = pe.matmul(PS[:, 4, j * D:(j + 1) * D], p3T[:, j, :], xv[:, j, :], start=True, stop=True)
                mm.then_inc(s_pv3, 1)
                if not first:
                    ffn_down(g - 1, [2, 3])
                pe.wait_ge(s_x3, 2 * g + 2)
                for j in range(NJ):
                    mm = pe.transpose(PS[:, 0, j * P:(j + 1) * P], x3[:, j, :], ident)
                mm.then_inc(s_x3T_mm, 1)

            group(0, first=True)
            group(1, second=True)
            with pe.Fori(2, T) as g:
                group(g)
            for c in range(FC):
                ffn_up(T - 1, c)
            ffn_down(T - 1, [0, 1, 2, 3])


def tables():
    c = np.zeros((P, C_END), np.float32)
    i = np.arange(P)
    c[:, C_ID:C_ID + P] = np.eye(P)
    c[:, C_TRI:C_TRI + P] = i[:, None] <= i[None, :]
    c[:, C_ONE:C_ONE + P] = 1
    c[:, C_BLK:C_BLK + P] = np.where(i[:, None] % SUB == i[None, :] % SUB, 0.0, -1e30)
    b, k, t = np.meshgrid(np.arange(B), np.arange(K), np.arange(T), indexing="ij")
    c[:, C_BASE:C_TRASH] = ((b // 2) * E * SLOTS + (b % 2) * CAP - 1).reshape(1, -1)
    c[:, C_TRASH:C_IOTA] = ROWS + ((b * K + k) * T + t).reshape(1, -1) * P + i[:, None]
    c[:, C_IOTA:C_END] = np.arange(E)
    s = np.arange(S, dtype=np.float32)
    g = np.exp(np.float32(-0.5) * ((s - np.float32(S / 2)) / np.float32(S / 4)) ** 2) / np.sqrt(np.float32(D))
    return c, np.ascontiguousarray(np.broadcast_to(g.astype(np.float32)[None, :], (P, S)))


def kernel(**inputs):
    import concourse.bacc as _bacc
    from concourse.bass_utils import run_bass_kernel_spmd as _run

    def a(name):
        return np.asarray(inputs[name])

    consts, gmask = tables()
    x = a("L0_attn_x").reshape(B * S, D)
    w1, w3 = a("L0_ffn_w1"), a("L0_ffn_w3")
    laid = {
        "xT": x.T, "x": x,
        "wqT": a("L0_attn_Wq").T, "wkT": a("L0_attn_Wk").T, "wv": a("L0_attn_Wv"), "woT": a("L0_attn_Wo").T,
        "bq": a("L0_attn_bq").reshape(D, 1), "bk": a("L0_attn_bk").reshape(D, 1), "bv": a("L0_attn_bv").reshape(D, 1),
        "bo": np.broadcast_to(a("L0_attn_bo").reshape(1, D), (P, D)),
        "gateT": a("L0_ffn_gate_w").T,
        "w13": np.concatenate([w1, w3[:, :, 3 * P:], w3[:, :, :3 * P]], axis=2),
        "w2": a("L0_ffn_w2"),
        "u1T": a("L1_ffn_U1").T, "v1": a("L1_ffn_V1"), "u2T": a("L1_ffn_U2").T, "v2": a("L1_ffn_V2"),
        "b1": a("L1_ffn_b1").reshape(FC, P).T, "b2": np.broadcast_to(a("L1_ffn_b2").reshape(1, D), (P, D)),
        "consts": consts, "gmask": gmask,
    }
    nc = _bacc.Bacc("TRN2", target_bir_lowering=False, num_devices=1)
    arrays, args = {}, []
    for name, v in laid.items():
        v = np.ascontiguousarray(v)
        arrays[f"in_{name}"] = v
        args.append(nc.dram_tensor(f"in_{name}", v.shape, mybir.dt.from_np(v.dtype), kind="ExternalInput").ap())
    args.append(nc.dram_tensor("out_0", (B, S, D), F32, kind="ExternalOutput").ap())
    build(nc, *args)
    r = _run(nc, [arrays], core_ids=[0])
    return r.results[0]["out_0"]
```

```python
from contextlib import ExitStack

import numpy as np

import concourse.bass as bass
from concourse import mybir

F32 = mybir.dt.float32
F32R = mybir.dt.float32r
U32 = mybir.dt.uint32
ALU = mybir.AluOpType
ACT = mybir.ActivationFunctionType
AX = mybir.AxisListType

P = 128
B, S, D = 4, 1024, 128
E, K, F = 8, 2, 448
CAP = int(S * K / E * 1.25)
DFF, RANK = 512, 32
EPS = 1e-5
T = S // P
NT = B * T
PAIRS = B // 2
SLOTS = 2 * CAP
Q = SLOTS // P
J = PAIRS * E
ROWS = J * SLOTS
FT = F - 3 * P
HALF = SLOTS // 2
NU = 8
SUB = 32
NJ = P // SUB
FC = DFF // P

C_ID, C_TRI, C_ONE, C_BLK = 0, P, 2 * P, 3 * P
C_BASE = 4 * P
C_TRASH = C_BASE + B * K * T
C_IOTA = C_TRASH + B * K * T
C_END = C_IOTA + E


class Steps:

    def __init__(self, eng, sem):
        self.eng, self.sem, self.n = eng, sem, 0

    def add(self, ins):
        ins.then_inc(self.sem, 1)
        self.n += 1

    def wait(self, back=0):
        self.eng.wait_ge(self.sem, self.n - back)

    def close(self):
        self.wait()
        self.eng.sem_clear(self.sem)
        self.n = 0


def live(n, count=T):
    return not isinstance(n, int) or 0 <= n < count


def after_first(n):
    return not isinstance(n, int) or n > 0


def build(nc, xT, x, wqT, wkT, wv, woT, bq, bk, bv, bo, gateT, w13, w2, u1T, v1, u2T, v2, b1, b2, consts, gmask, out):
    ctx = ExitStack()
    with ctx:
        def sb(name, shape, dt=F32):
            return ctx.enter_context(nc.sbuf_tensor(name, shape, dt))

        def sem(name):
            return ctx.enter_context(nc.semaphore(name))

        x_slots = nc.dram_tensor("x_slots", (ROWS + NT * P * K, D), F32, kind="Internal").ap()
        y_slots = nc.dram_tensor("y_slots", (ROWS, D), F32, kind="Internal").ap()

        cst = sb("cst", [P, C_END])
        ident, tri, ones = cst[:, C_ID:C_ID + P], cst[:, C_TRI:C_TRI + P], cst[:, C_ONE:C_ONE + P]
        blockmask = cst[:, C_BLK:C_BLK + P]
        base_tab = cst[:, C_BASE:C_TRASH].rearrange("p (b n) -> p b n", b=B)
        trash_tab = cst[:, C_TRASH:C_IOTA].rearrange("p (b n) -> p b n", b=B)
        iota = cst[:, C_IOTA:C_END]
        gm = sb("gm", [P, S])
        wqT_s, wkT_s, wv_s, woT_s = (sb(n, [P, D]) for n in ("wqT_s", "wkT_s", "wv_s", "woT_s"))
        wvoT_s = sb("wvoT_s", [P, D])
        bq_s, bk_s, bv_s = sb("bq_s", [P, 1]), sb("bk_s", [P, 1]), sb("bv_s", [P, 1])
        bv_wide = sb("bv_wide", [P, P])
        bo_s, beff = sb("bo_s", [P, D]), sb("beff", [P, D])
        gateT_s = sb("gateT_s", [P, E])
        u1T_s, v1_s = sb("u1T_s", [RANK, D]), sb("v1_s", [RANK, DFF])
        u2T_s, v2_s = sb("u2T_s", [RANK, DFF]), sb("v2_s", [RANK, D])
        f1_s, f2_s = sb("f1_s", [P, DFF]), sb("f2_s", [P, FC, D])
        b1_s, b2_s = sb("b1_s", [P, FC]), sb("b2_s", [P, D])
        zeros = sb("zeros", [P, 2560])
        mhalf = sb("mhalf", [P, T])

        xT_s, xn_s, xb_s = sb("xT_s", [P, S]), sb("xn_s", [P, T, D]), sb("xb_s", [P, T, D])
        QT, KT, V = sb("QT", [P, S]), sb("KT", [P, S]), sb("V", [P, T, D])
        prob = sb("prob", [P, 2, S])
        PT = sb("PT", [P, T, P])
        nmax, rsum, rinv = sb("nmax", [P, T]), sb("rsum", [P, T]), sb("rinv", [P, T])
        h1 = sb("h1", [P, T, D])
        st1, mv1 = sb("st1", [P, T, 6]), sb("mv1", [P, T, 2])
        ve1, rs1 = sb("ve1", [P, T]), sb("rs1", [P, T])
        x1b = sb("x1b", [P, T, D])
        x1_all = sb("x1_all", [P, NT, D])
        x1T = sb("x1T", [P, S])
        lg, lmx, lsh, lex = sb("lg", [P, T, E]), sb("lmx", [P, T]), sb("lsh", [P, T, E]), sb("lex", [P, T, E])
        lsum, linv, pr = sb("lsum", [P, T]), sb("linv", [P, T]), sb("pr", [P, T, E])
        top, tix = sb("top", [P, T, E]), sb("tix", [P, T, E], U32)
        tixf = sb("tixf", [P, K, T])
        oh = sb("oh", [P, K, T, E])
        both = sb("both", [P, T, E])
        before = sb("before", [P, T, E])
        cnt = sb("cnt", [P, T, E])
        ohc = sb("ohc", [P, K, T, E])
        pos, fits, slot = sb("pos", [P, K, T]), sb("fits", [P, K, T]), sb("slot", [P, K, T])
        row_g, row_d = sb("row_g", [P, K * T]), sb("row_d", [P, K * T])
        row_s = sb("row_s", [P, K * T])
        sidx = sb("sidx", [P, K * T], U32)
        gidx = sb("gidx", [P, B, K * T], U32)
        wts = sb("wts", [P, B, K * T])
        Xn = sb("Xn", [P, 2, Q * D])
        XTh, XTl = sb("XTh", [P, 2, SLOTS], F32R), sb("XTl", [P, 2, SLOTS], F32R)
        w13_s = sb("w13_s", [P, 2, 2 * F])
        w13h, w13l = sb("w13h", [P, 2, 2 * F], F32R), sb("w13l", [P, 2, 2 * F], F32R)
        w2_s = sb("w2_s", [P, 2, 4, D])
        sil = sb("sil", [P, 2, HALF])
        G = sb("G", [P, 2, 4, SLOTS])
        Ys = sb("Ys", [P, 2, Q * D])
        gi_s, wt_s = sb("gi_s", [P, 2 * K], U32), sb("wt_s", [P, 2 * K])
        GA = sb("GA", [P, 2 * K, D])
        nb2 = sb("nb2", [P, B])
        x2 = sb("x2", [P, B, D])
        st2, mv2, ve2, rs2 = sb("st2", [P, B, 6]), sb("mv2", [P, B, 2]), sb("ve2", [P, B]), sb("rs2", [P, B])
        x2T = sb("x2T", [P, NJ, B * SUB])
        xv = sb("xv", [P, NJ, D])
        sm = sb("sm", [P, NJ, P])
        nm3, sum3, inv3 = sb("nm3", [P, NJ]), sb("sum3", [P, NJ]), sb("inv3", [P, NJ])
        p3, p3T = sb("p3", [P, NJ, P]), sb("p3T", [P, NJ, P])
        h3 = sb("h3", [P, NJ, D])
        st3, mv3, ve3, rs3 = sb("st3", [P, NJ, 6]), sb("mv3", [P, NJ, 2]), sb("ve3", [P, NJ]), sb("rs3", [P, NJ])
        x3, x3b = sb("x3", [P, NJ, D]), sb("x3b", [P, NJ, D])
        x3T = sb("x3T", [P, NJ * P])
        H = sb("H", [P, FC, NJ * P])
        h4 = sb("h4", [P, NJ, D])
        st4, mv4, ve4, rs4 = sb("st4", [P, NJ, 6]), sb("mv4", [P, NJ, 2]), sb("ve4", [P, NJ]), sb("rs4", [P, NJ])
        x4 = sb("x4", [P, NJ, D])

        PS = ctx.enter_context(nc.psum_tensor("PS", [P, 8, 512], F32))

        s_ld0 = sem("s_ld0")
        s_ld1 = sem("s_ld1")
        s_xT = sem("s_xT")
        s_xn = sem("s_xn")
        s_zero = sem("s_zero")
        s_x1all = sem("s_x1all")
        s_Xn = [sem("s_Xn0"), sem("s_Xn1")]
        s_w13 = [sem("s_w130"), sem("s_w131")]
        s_w = [sem("s_w0"), sem("s_w1")]
        s_yst = [sem("s_yst0"), sem("s_yst1")]
        s_out = sem("s_out")
        s_init = sem("s_init")
        s_xb = sem("s_xb")
        s_rs1 = sem("s_rs1")
        s_sc = sem("s_sc")
        s_pool = sem("s_pool")
        s_ga = sem("s_ga")
        s_rs2, s_rs3, s_rs4 = sem("s_rs2"), sem("s_rs3"), sem("s_rs4")
        s_prep_mm = sem("s_prep_mm")
        s_prep_ev = sem("s_prep_ev")
        s_bvw = sem("s_bvw")
        s_k_mm, s_q_mm, s_v_mm = sem("s_k_mm"), sem("s_q_mm"), sem("s_v_mm")
        s_k_ev, s_q_ev = sem("s_k_ev"), sem("s_q_ev")
        s_v0_ev, s_v1_ev = sem("s_v0_ev"), sem("s_v1_ev")
        s_s = sem("s_s")
        s_max = sem("s_max")
        s_exp = sem("s_exp")
        s_t = sem("s_t")
        s_e0, s_e1 = sem("s_e0"), sem("s_e1")
        s_pv = sem("s_pv")
        s_o = sem("s_o")
        s_own = sem("s_own")
        s_var1 = sem("s_var1")
        s_x1 = sem("s_x1")
        s_r_mm = sem("s_r_mm")
        s_r_ev = sem("s_r_ev")
        s_lsh = sem("s_lsh")
        s_lex = sem("s_lex")
        s_both = sem("s_both")
        s_idx = sem("s_idx")
        s_XT_mm = sem("s_XT_mm")
        s_XTh, s_XTl = sem("s_XTh"), sem("s_XTl")
        s_wh, s_wl = sem("s_wh"), sem("s_wl")
        s_ha = sem("s_ha")
        s_h = sem("s_h")
        s_sil = sem("s_sil")
        s_g = sem("s_g")
        s_y = sem("s_y")
        s_ye = sem("s_ye")
        s_comb = sem("s_comb")
        s_nb2 = sem("s_nb2")
        s_var2, s_var3, s_var4 = sem("s_var2"), sem("s_var3"), sem("s_var4")
        s_x2 = sem("s_x2")
        s_x2T_mm, s_x2T_ev = sem("s_x2T_mm"), sem("s_x2T_ev")
        s_xv_mm, s_xv_ev = sem("s_xv_mm"), sem("s_xv_ev")
        s_s3 = sem("s_s3")
        s_sm = sem("s_sm")
        s_p3 = sem("s_p3")
        s_p3T_mm, s_p3T_ev = sem("s_p3T_mm"), sem("s_p3T_ev")
        s_pv3 = sem("s_pv3")
        s_h3 = sem("s_h3")
        s_x3 = sem("s_x3")
        s_x3b = sem("s_x3b")
        s_x3T_mm, s_x3T_ev = sem("s_x3T_mm"), sem("s_x3T_ev")
        s_f1 = sem("s_f1")
        s_gelu = sem("s_gelu")
        s_f2 = sem("s_f2")
        s_h4 = sem("s_h4")
        s_x4 = sem("s_x4")

        block = ctx.enter_context(nc.Block())

        @block.sync
        def _(sp):
            def load(dst, src, s):
                sp.dma_start(dst, src).then_inc(s, 16)

            load(wkT_s[:, :], wkT, s_ld0)
            load(xT_s[:, :], xT[:, 0:S], s_xT)
            load(wqT_s[:, :], wqT, s_ld0)
            load(wv_s[:, :], wv, s_ld0)
            load(woT_s[:, :], woT, s_ld0)
            load(gm[:, :], gmask, s_ld0)
            load(cst[:, :], consts, s_ld0)
            load(bq_s[:, :], bq, s_ld0)
            load(bk_s[:, :], bk, s_ld0)
            load(bv_s[:, :], bv, s_ld0)
            load(bo_s[:, :], bo, s_ld0)
            load(gateT_s[:, :], gateT, s_ld0)
            load(b1_s[:, :], b1, s_ld0)
            load(b2_s[:, :], b2, s_ld0)
            load(xn_s[:, :, :], x[0:S, :].rearrange("(t p) d -> p t d", p=P), s_xn)
            load(u1T_s[:, :], u1T, s_ld1)
            load(v1_s[:, :], v1, s_ld1)
            load(u2T_s[:, :], u2T, s_ld1)
            load(v2_s[:, :], v2, s_ld1)
            sp.wait_ge(s_init, 1)
            zr = x_slots[0:ROWS, :].rearrange("(q p t) d -> q p (t d)", p=P, t=2560 // D)
            for q in range(zr.shape[0]):
                load(zr[q], zeros[:, :], s_zero)

            def up_weights(j, u):
                load(w13_s[:, u, :], w13[bass.ds(j % E, 1), :, :].rearrange("e p n -> p (e n)"), s_w13[u])

            def down_weights(j, u):
                load(w2_s[:, u, 0:3, :], w2[bass.ds(j % E, 1), 0:3 * P, :].rearrange("e (c p) d -> p (e c) d", p=P), s_w[u])
                load(w2_s[0:FT, u, 3, :], w2[bass.ds(j % E, 1), 3 * P:F, :].rearrange("e p d -> p (e d)"), s_w[u])

            with sp.Fori(0, B - 1) as b:
                sp.wait_ge(s_v_mm, 2 * b + 2)
                load(xT_s[:, :], xT[:, bass.ds((b + 1) * S, S)], s_xT)
                sp.wait_ge(s_xb, b + 1)
                load(xn_s[:, :, :], x[bass.ds((b + 1) * S, S), :].rearrange("(t p) d -> p t d", p=P), s_xn)
                sp.wait_ge(s_x1, b + 1)
                load(x1_all[:, bass.ds(b * T, T), :], x1b[:, :, :], s_x1all)
            for j in range(2):
                up_weights(j, j)
                down_weights(j, j)

            def slots_in(j, u):
                load(Xn[:, u, :], x_slots[bass.ds(j * SLOTS, SLOTS), :].rearrange("(p t) d -> p (t d)", p=P), s_Xn[u])

            def slots_out(j, u):
                sp.wait_ge(s_ye, j + 1)
                load(y_slots[bass.ds(j * SLOTS, SLOTS), :].rearrange("(p t) d -> p (t d)", p=P), Ys[:, u, :], s_yst[u])

            slots_in(0, 0)
            slots_in(1, 1)
            sp.wait_ge(s_x1, B)
            load(x1_all[:, (B - 1) * T:NT, :], x1b[:, :, :], s_x1all)
            with sp.Fori(0, J // 2 - 1) as i:
                for u in range(2):
                    j = 2 * i + u
                    sp.wait_ge(s_wl, j + 1)
                    up_weights(j + 2, u)
                    sp.wait_ge(s_XT_mm, j + 1)
                    if u == 0:
                        sp.wait_ge(s_sc, 16 * K * T * (B - 1 + (i + 1) // (J // 4)))
                    slots_in(j + 2, u)
                    sp.wait_ge(s_y, j + 1)
                    down_weights(j + 2, u)
                    slots_out(j, u)
            slots_out(J - 2, 0)
            slots_out(J - 1, 1)

            def output(g):
                sp.wait_ge(s_x4, g + 1)
                for b in range(B):
                    load(out[b, bass.ds(g * P, P), :].rearrange("(j s) d -> s j d", s=SUB),
                         x4[b * SUB:(b + 1) * SUB, :, :], s_out)

            with sp.Fori(0, T) as g:
                output(g)
            sp.wait_ge(s_out, 16 * B * T)

        @block.gpsimd
        def _(pool):
            own = Steps(pool, s_pool)
            pool.memset(zeros[:, :], 0.0).then_inc(s_init, 1)
            pool.memset(mhalf[:, :], -0.5).then_inc(s_init, 1)

            def x_plus_bias(b):
                if not isinstance(b, int) or b > 0:
                    pool.wait_ge(s_o, T * b)
                else:
                    pool.wait_ge(s_prep_ev, 2)
                pool.wait_ge(s_xn, 16 * b + 16)
                pool.tensor_tensor(xb_s[:, :, :], xn_s[:, :, :], beff[:, None, :].to_broadcast([P, T, D]),
                                   ALU.add).then_inc(s_xb, 1)

            def scatter(r):
                pool.wait_ge(s_zero, 16 * (ROWS * D // (P * 2560)))
                pool.wait_ge(s_idx, r + 1)
                pool.engine_nop()
                for k in range(K):
                    for t in range(T):
                        pool.indirect_dma_start(x_slots[:, :], bass.IndirectOffsetOnAxis(ap=sidx[:, k * T + t:k * T + t + 1], axis=0),
                                                x1b[:, t, :], None).then_inc(s_sc, 16)

            def rstd1(b):
                pool.wait_ge(s_var1, b + 1)
                pool.tensor_tensor(rs1[:, :], ve1[:, :], mhalf[:, :], ALU.pow).then_inc(s_rs1, 1)

            pool.wait_ge(s_init, 2)
            x_plus_bias(0)
            rstd1(0)
            with pool.Fori(1, B) as b:
                x_plus_bias(b)
                scatter(b - 1)
                rstd1(b)
            scatter(B - 1)

            def gather(pair, g):
                n = pair * T + g
                if after_first(n):
                    pool.wait_ge(s_comb, n)
                for src, dst in ((gidx, gi_s), (wts, wt_s)):
                    own.add(pool.tensor_copy(dst[:, :], src[:, 2 * pair:2 * pair + 2, :].rearrange("p b (k t) -> p (b k) t", k=K)[:, :, g]))
                own.close()
                for i in range(2 * K):
                    pool.indirect_dma_start(GA[:, i, :], None, y_slots[0:(pair + 1) * E * SLOTS, :],
                                            bass.IndirectOffsetOnAxis(ap=gi_s[:, i:i + 1], axis=0)).then_inc(s_ga, 16)

            def rstd(n, var, s_var, r, s_rs):
                pool.wait_ge(s_var, n + 1)
                pool.tensor_tensor(r[:, :], var[:, :], mhalf[:, 0:NJ], ALU.pow).then_inc(s_rs, 1)

            for u in range(2):
                pool.wait_ge(s_yst[u], 16 * (E // 2))
            with pool.Fori(0, T) as g:
                gather(0, g)
            for u in range(2):
                pool.wait_ge(s_yst[u], 16 * (J // 2))
            gather(1, 0)

            def group(g):
                if live(g + 1):
                    rstd(g + 1, ve2, s_var2, rs2, s_rs2)
                if live(g + 2):
                    gather(1, g + 2)
                if live(g - 2):
                    rstd(g - 2, ve4, s_var4, rs4, s_rs4)
                if live(g):
                    rstd(g, ve3, s_var3, rs3, s_rs3)

            for g in range(-1, 2):
                group(g)
            with pool.Fori(2, T - 2) as g:
                group(g)
            for g in range(T - 2, T + 2):
                group(g)

        @block.scalar
        def _(act):
            def exps(g, t):
                act.wait_ge(s_max, g + 1)
                act.activation(prob[:, t % 2, :].rearrange("p (h n) -> p h n", h=2), PS[:, 2 * (t % 2):2 * (t % 2) + 2, :], ACT.Exp,
                               bias=nmax[:, t:t + 1], accum_out=rsum[:, t:t + 1]).then_inc(s_exp, 1)

            def q_out(b):
                act.wait_ge(s_q_mm, b + 1)
                act.activation(QT[:, :].rearrange("p (h n) -> p h n", h=2), PS[:, 2:4, :], ACT.Identity, bias=bq_s[:, 0:1]).then_inc(s_q_ev, 1)

            def v_out(b):
                act.wait_ge(s_v_mm, 2 * b + 1)
                act.activation(V[:, 0:4, :], PS[:, 4, :].rearrange("p (t d) -> p t d", t=4), ACT.Copy).then_inc(s_v0_ev, 1)

            def router_out(r, n, dst, cols, bank=7):
                act.wait_ge(s_r_mm, 4 * r + n + 1)
                act.activation(dst, PS[:, bank, 0:cols], ACT.Copy).then_inc(s_r_ev, 1)

            def router_exp(r):
                act.wait_ge(s_lsh, r + 1)
                act.activation(lex[:, :, :], lsh[:, :, :], ACT.Exp).then_inc(s_lex, 1)

            def body(b, first=False, last=False):
                for t in range(T):
                    g = b * T + t
                    act.wait_ge(s_t, 2 * g + 1)
                    act.activation(PT[:, 0:4, :], PS[:, 4, :].rearrange("p (k n) -> p k n", k=4), ACT.Copy).then_inc(s_e0, 1)
                    if t == 1 and not first:
                        router_out(b - 1, 1, x1T[:, 512:1024], 512)
                    if t + 2 < T:
                        exps(g + 2, t + 2)
                    if t == 0 and not first:
                        router_out(b - 1, 0, x1T[:, 0:512], 512)
                    if t == 1 and not first:
                        router_out(b - 1, 2, lg[:, :, :].rearrange("p t e -> p (t e)"), T * E)
                    if t == 2 and not first:
                        router_exp(b - 1)
                    if t == 4 and not first:
                        router_out(b - 1, 3, cnt[:, :, :].rearrange("p t e -> p (t e)"), T * E)
                if not last:
                    q_out(b + 1)
                    v_out(b + 1)
                    exps(b * T + T, 0)
                    exps(b * T + T + 1, 1)

            act.wait_ge(s_ld0, 16 * 13)
            q_out(0)
            v_out(0)
            exps(0, 0)
            exps(1, 1)
            body(0, first=True)
            with act.Fori(1, B - 1) as b:
                body(b)
            body(B - 1, last=True)

            def slots_T(j, u):
                act.wait_ge(s_XT_mm, j + 1)
                act.activation(XTh[:, u, 0:512], PS[:, 0, :], ACT.Copy)
                act.activation(XTh[:, u, 512:SLOTS], PS[:, 1, 0:SLOTS - 512], ACT.Copy).then_inc(s_XTh, 1)

            def w13_high(j, u, n):
                act.wait_ge(s_w13[u], 16 * (n + 1))
                act.activation(w13h[:, u, :], w13_s[:, u, :], ACT.Copy).then_inc(s_wh, 1)

            def silu(j, k):
                act.wait_ge(s_ha, NU * j + k + 1)
                n = P if k < 6 else FT
                act.activation(sil[0:n, k % 2, :], PS[0:n, 2 + 2 * (k % 2), 0:HALF], ACT.Silu).then_inc(s_sil, 1)

            def pass_(j, u, m, between=lambda k: None):
                for k in range(2, NU):
                    if k == 4 and live(j + 1, J):
                        w13_high(j + 1, 1 - u, m)
                    if k == 6 and live(j + 1, J):
                        slots_T(j + 1, 1 - u)
                    silu(j, k)
                    between(k)
                if live(j + 1, J):
                    silu(j + 1, 0)
                    silu(j + 1, 1)

            def router_parts(k):
                if k == 5:
                    router_out(B - 1, 0, x1T[:, 0:512], 512)
                if k == 7:
                    router_out(B - 1, 1, x1T[:, 512:1024], 512)

            w13_high(0, 0, 0)
            slots_T(0, 0)
            silu(0, 0)
            silu(0, 1)
            pass_(0, 0, 0, router_parts)
            router_out(B - 1, 2, lg[:, :, :].rearrange("p t e -> p (t e)"), T * E)
            router_exp(B - 1)
            pass_(1, 1, 1)
            router_out(B - 1, 3, cnt[:, :, :].rearrange("p t e -> p (t e)"), T * E, bank=1)
            with act.Fori(1, J // 2 - 1) as i:
                pass_(2 * i, 0, i)
                pass_(2 * i + 1, 1, i + 1)
            pass_(J - 2, 0, J // 2 - 1)
            pass_(J - 1, 1, J // 2)

            def gelu(g, c):
                act.wait_ge(s_f1, FC * g + c + 1)
                act.activation(H[:, c, :], PS[:, 5 + c % 2, :], ACT.Gelu_apprx_tanh, bias=b1_s[:, c:c + 1]).then_inc(s_gelu, 1)

            def copy_out(mm, n, dst, bank, ev):
                act.wait_ge(mm, n)
                act.activation(dst, PS[:, bank, :].rearrange("p (k n) -> p k n", k=4), ACT.Copy).then_inc(ev, 1)

            def group(g):
                if live(g):
                    if after_first(g):
                        act.wait_ge(s_h3, g)
                    copy_out(s_xv_mm, g + 1, xv[:, :, :], 1, s_xv_ev)
                    act.wait_ge(s_sm, 2 * g + 2)
                    for j in range(NJ):
                        act.activation(p3[:, j, :], sm[:, j, :], ACT.Exp, bias=nm3[:, j:j + 1],
                                       accum_out=sum3[:, j:j + 1]).then_inc(s_p3, 1)
                    copy_out(s_p3T_mm, g + 1, p3T[:, :, :], 3, s_p3T_ev)
                if live(g - 1):
                    copy_out(s_x3T_mm, g, x3T[:, :].rearrange("p (k n) -> p k n", k=4), 0, s_x3T_ev)
                    gelu(g - 1, 0)
                    gelu(g - 1, 1)
                if live(g + 1):
                    act.wait_ge(s_nb2, g + 2)
                    for b in range(B):
                        ins = act.activation(x2[:, b, :], x1_all[:, bass.ds(b * T + g + 1, 1), :].rearrange("p o d -> p (o d)"), ACT.Identity,
                                             bias=nb2[:, b:b + 1], scale=rs2[:, b:b + 1])
                    ins.then_inc(s_x2, 1)
                if live(g - 1):
                    gelu(g - 1, 2)
                    gelu(g - 1, 3)
                if live(g + 1):
                    act.wait_ge(s_x2T_mm, g + 2)
                    act.activation(x2T[:, :, :].rearrange("p j (b s) -> p b j s", b=B), PS[:, 0, :].rearrange("p (b j s) -> p b j s", b=B, j=NJ),
                                   ACT.Copy).then_inc(s_x2T_ev, 1)

            for g in range(-1, 2):
                group(g)
            with act.Fori(2, T - 1) as g:
                group(g)
            for g in range(T - 1, T + 1):
                group(g)

        @block.vector
        def _(dve):
            own = Steps(dve, s_own)

            def k_out(b):
                dve.wait_ge(s_k_mm, b + 1)
                dve.scalar_tensor_tensor(out=KT[:, :].rearrange("p (h n) -> p h n", h=2), in0=PS[:, 0:2, :],
                                         scalar=bk_s[:, 0:1], in1=gm[:, :].rearrange("p (h n) -> p h n", h=2),
                                         op0=ALU.add, op1=ALU.mult).then_inc(s_k_ev, 1)

            def v_out(b):
                dve.wait_ge(s_v_mm, 2 * b + 2)
                dve.tensor_copy(V[:, 4:8, :], PS[:, 5, :].rearrange("p (t d) -> p t d", t=4)).then_inc(s_v1_ev, 1)

            def row_max(g, t):
                dve.wait_ge(s_s, g + 1)
                dve.tensor_reduce(nmax[:, t:t + 1], PS[:, 2 * (t % 2):2 * (t % 2) + 2, :], AX.XY, ALU.max, negate=True).then_inc(s_max, 1)

            def residual(g, t):
                dve.wait_ge(s_exp, g + 1)
                own.add(dve.reciprocal(rinv[:, t:t + 1], rsum[:, t:t + 1]))
                dve.wait_ge(s_pv, g + 1)
                own.wait()
                dve.scalar_tensor_tensor(out=h1[:, t, :], in0=PS[:, 6, 0:D], scalar=rinv[:, t:t + 1],
                                         in1=xb_s[:, t, :], op0=ALU.mult, op1=ALU.add).then_inc(s_o, 1)
                dve.wait_ge(s_o, g + 1)
                own.add(dve.bn_stats(st1[:, t, :], h1[:, t, :]))
                own.wait()
                own.add(dve.bn_aggr(mv1[:, t, :], st1[:, t, :]))

            def var1(b):
                own.wait()
                dve.tensor_scalar(ve1[:, :], mv1[:, :, 1], EPS, None, ALU.add).then_inc(s_var1, 1)

            def ln1(b, first=False):
                dve.wait_ge(s_rs1, b + 1)
                if not first:
                    dve.wait_ge(s_sc, 16 * K * T * b)
                    dve.wait_ge(s_x1all, 16 * b)
                for t in range(T):
                    ins = dve.tensor_scalar(x1b[:, t, :], h1[:, t, :], mv1[:, t, 0:1], rs1[:, t:t + 1], ALU.subtract, ALU.mult)
                ins.then_inc(s_x1, 1)

            def router_shift(r):
                dve.wait_ge(s_r_ev, 4 * r + 3)
                own.add(dve.tensor_reduce(lmx[:, :], lg[:, :, :], AX.X, ALU.max))
                own.wait()
                dve.tensor_tensor(lsh[:, :, :], lg[:, :, :], lmx[:, :, None].to_broadcast([P, T, E]), ALU.subtract).then_inc(s_lsh, 1)

            def router_top(r):
                dve.wait_ge(s_lex, r + 1)
                own.add(dve.tensor_reduce(lsum[:, :], lex[:, :, :], AX.X, ALU.add))
                own.wait()
                own.add(dve.reciprocal(linv[:, :], lsum[:, :]))
                own.wait()
                own.add(dve.tensor_tensor(pr[:, :, :], lex[:, :, :], linv[:, :, None].to_broadcast([P, T, E]), ALU.mult))
                own.wait()
                for t in range(T):
                    own.add(dve.max(top[:, t, :], pr[:, t, :]))
                for t in range(T):
                    own.wait(back=T - 1)
                    own.add(dve.max_index(tix[:, t, :], top[:, t, :], pr[:, t, :]))
                own.wait()
                own.add(dve.tensor_copy(tixf[:, :, :], tix[:, :, 0:K].rearrange("p t k -> p k t")))

            def router_choice(r):
                own.wait()
                own.add(dve.tensor_tensor(oh[:, :, :, :].rearrange("p k t e -> p (k t) e"),
                                          tixf[:, :, :].rearrange("p k t -> p (k t)")[:, :, None].to_broadcast([P, K * T, E]),
                                          iota[:, None, :].to_broadcast([P, K * T, E]), ALU.is_equal))
                own.wait()
                own.add(dve.tensor_tensor(both[:, :, :], oh[:, 0, :, :], oh[:, 1, :, :], ALU.add))
                own.add(dve.memset(before[:, 0, :], 0.0))
                for t in range(1, T):
                    own.wait()
                    ins = dve.tensor_tensor(before[:, t, :], before[:, t - 1, :], both[:, t - 1, :], ALU.add)
                    if t < T - 1:
                        own.add(ins)
                ins.then_inc(s_both, 1)

            def router_rows(r):
                dve.wait_ge(s_r_ev, 4 * r + 4)
                own.add(dve.tensor_tensor(ohc[:, :, :, :], oh[:, :, :, :], cnt[:, None, :, :].to_broadcast([P, K, T, E]), ALU.mult))
                own.wait()
                own.add(dve.tensor_reduce(pos[:, :, :].rearrange("p k t -> p (k t)"), ohc[:, :, :, :].rearrange("p k t e -> p (k t) e"), AX.X, ALU.add))
                own.wait()
                own.add(dve.tensor_scalar(fits[:, :, :], pos[:, :, :], float(CAP), None, ALU.is_le))
                own.add(dve.tensor_scalar(slot[:, :, :], pos[:, :, :], float(CAP), None, ALU.min))
                own.wait()
                own.add(dve.scalar_tensor_tensor(out=row_d[:, :], in0=tixf[:, :, :].rearrange("p k t -> p (k t)"), scalar=float(SLOTS),
                                                 in1=slot[:, :, :].rearrange("p k t -> p (k t)"), op0=ALU.mult, op1=ALU.add))
                own.wait()
                own.add(dve.tensor_tensor(row_g[:, :], row_d[:, :], base_tab[:, r, :], ALU.add))
                own.wait()
                own.add(dve.tensor_tensor(row_d[:, :], row_g[:, :], trash_tab[:, r, :], ALU.subtract))
                own.wait()
                own.add(dve.tensor_tensor(row_s[:, :], row_d[:, :], fits[:, :, :].rearrange("p k t -> p (k t)"), ALU.mult))
                own.wait()
                own.add(dve.tensor_tensor(row_d[:, :], row_s[:, :], trash_tab[:, r, :], ALU.add))
                own.wait()
                dve.tensor_copy(gidx[:, r, :], row_g[:, :])
                dve.tensor_tensor(wts[:, r, :].rearrange("p (k t) -> p k t", k=K), top[:, :, 0:K].rearrange("p t k -> p k t"),
                                  fits[:, :, :], ALU.mult)
                dve.tensor_copy(sidx[:, :], row_d[:, :]).then_inc(s_idx, 1)

            def body(b, first=False, last=False):
                for t in range(T):
                    g = b * T + t
                    dve.wait_ge(s_t, 2 * g + 2)
                    dve.tensor_copy(PT[:, 4:8, :], PS[:, 5, :].rearrange("p (k n) -> p k n", k=4)).then_inc(s_e1, 1)
                    if t == 2 and not first:
                        router_shift(b - 1)
                    if t + 2 < T:
                        row_max(g + 2, t + 2)
                    if t == 0:
                        dve.wait_ge(s_xb, b + 1)
                    residual(g, t)
                    if t == 2 and not first:
                        router_top(b - 1)
                    if t == 3 and not first:
                        router_choice(b - 1)
                    if t == 4 and not first:
                        router_rows(b - 1)
                    if t == 6 and not last:
                        k_out(b + 1)
                var1(b)
                if not last:
                    v_out(b + 1)
                    row_max(b * T + T, 0)
                    row_max(b * T + T + 1, 1)
                if not last:
                    ln1(b, first)
                    own.close()

            dve.wait_ge(s_ld0, 16 * 13)
            dve.tensor_copy(bv_wide[:, :], bv_s[:, 0:1].to_broadcast([P, P])).then_inc(s_bvw, 1)
            k_out(0)
            dve.wait_ge(s_prep_mm, 1)
            dve.tensor_copy(wvoT_s[:, :], PS[:, 6, 0:D]).then_inc(s_prep_ev, 1)
            dve.wait_ge(s_prep_mm, 2)
            dve.tensor_tensor(beff[:, :], PS[:, 7, 0:D], bo_s[:, :], ALU.add).then_inc(s_prep_ev, 1)
            v_out(0)
            row_max(0, 0)
            row_max(1, 1)
            dve.wait_ge(s_prep_mm, 3)
            dve.tensor_copy(f1_s[:, :], PS[:, 6, :]).then_inc(s_prep_ev, 1)
            dve.wait_ge(s_prep_mm, 4)
            dve.tensor_copy(f2_s[:, :, :], PS[:, 7, :].rearrange("p (c d) -> p c d", c=FC)).then_inc(s_prep_ev, 1)
            body(0, first=True)
            with dve.Fori(1, B - 1) as b:
                body(b)
            body(B - 1, last=True)
            def gated(j, u, k):
                dve.wait_ge(s_sil, NU * j + k + 1)
                if k < 6:
                    dve.wait_ge(s_h, 6 * j + k + 1)
                c, h = k // 2, k % 2
                if c < 3:
                    dve.tensor_tensor(G[:, u, c, h * HALF:(h + 1) * HALF], sil[:, k % 2, :], PS[:, 3 + 2 * (k % 2), 0:HALF],
                                      ALU.mult).then_inc(s_g, 1)
                else:
                    dve.tensor_tensor(G[0:FT, u, c, h * HALF:(h + 1) * HALF], sil[0:FT, k % 2, :], PS[FT:2 * FT, 2 + 2 * (k % 2), 0:HALF],
                                      ALU.mult).then_inc(s_g, 1)

            def combine(pair, g):
                n = pair * T + g
                dve.wait_ge(s_ga, 16 * 2 * K * (n + 1))
                for k in range(K):
                    for b in range(2):
                        h = x1_all[:, bass.ds((2 * pair + b) * T + g, 1), :].rearrange("p o d -> p (o d)")
                        if k:
                            own.wait(back=1 - b)
                        ins = dve.scalar_tensor_tensor(out=h, in0=GA[:, K * b + k, :], scalar=wt_s[:, K * b + k:K * b + k + 1], in1=h,
                                                       op0=ALU.mult, op1=ALU.add)
                        if k == 0:
                            own.add(ins)
                ins.then_inc(s_comb, 1)

            def w13_low(j, u):
                dve.wait_ge(s_wh, j + 1)
                dve.tensor_tensor(w13l[:, u, :], w13_s[:, u, :], w13h[:, u, :].bitcast(F32), ALU.subtract).then_inc(s_wl, 1)

            def slots_low(j, u):
                dve.wait_ge(s_XTh, j + 1)
                dve.tensor_tensor(XTl[:, u, 0:512], PS[:, 0, :], XTh[:, u, 0:512].bitcast(F32), ALU.subtract)
                dve.tensor_tensor(XTl[:, u, 512:SLOTS], PS[:, 1, 0:SLOTS - 512], XTh[:, u, 512:SLOTS].bitcast(F32), ALU.subtract).then_inc(s_XTl, 1)

            def pass_(j, u, stored, between=lambda k: None):
                for k in range(2, NU):
                    if k == 4 and live(j + 1, J):
                        w13_low(j + 1, 1 - u)
                    if k == 6 and live(j + 1, J):
                        slots_low(j + 1, 1 - u)
                    gated(j, u, k)
                    between(k)
                if live(j + 1, J):
                    gated(j + 1, 1 - u, 0)
                    gated(j + 1, 1 - u, 1)
                dve.wait_ge(s_y, j + 1)
                if after_first(stored):
                    dve.wait_ge(s_yst[u], 16 * stored)
                dve.tensor_copy(Ys[:, u, 0:512], PS[:, 6, :])
                dve.tensor_copy(Ys[:, u, 512:Q * D], PS[:, 7, 0:Q * D - 512]).then_inc(s_ye, 1)

            def ln1_part(k):
                if k == 3:
                    ln1(B - 1)

            def router_parts(k):
                if k == 3:
                    router_top(B - 1)
                if k == 5:
                    router_choice(B - 1)

            w13_low(0, 0)
            slots_low(0, 0)
            gated(0, 0, 0)
            gated(0, 0, 1)
            pass_(0, 0, 0, ln1_part)
            router_shift(B - 1)
            pass_(1, 1, 0, router_parts)
            router_rows(B - 1)
            own.close()
            with dve.Fori(1, E // 2) as i:
                pass_(2 * i, 0, i)
                pass_(2 * i + 1, 1, i)
            dve.wait_ge(s_x1all, 16 * B)

            def pass_and_combine(i, u):
                pass_(2 * i + u, u, i)
                combine(0, 2 * (i - E // 2) + u)

            with dve.Fori(E // 2, J // 2 - 1) as i:
                pass_and_combine(i, 0)
                pass_and_combine(i, 1)
                own.close()
            pass_and_combine(J // 2 - 1, 0)
            pass_and_combine(J // 2 - 1, 1)
            own.close()

            def stats(h, st, mv, ve, s_var):
                for j in range(NJ):
                    own.add(dve.bn_stats(st[:, j, :], h(j)))
                for j in range(NJ):
                    own.wait(back=NJ - 1)
                    own.add(dve.bn_aggr(mv[:, j, :], st[:, j, :]))
                own.wait()
                dve.tensor_scalar(ve[:, :], mv[:, :, 1], EPS, None, ALU.add).then_inc(s_var, 1)

            def normal(h, mv, rs, xo, s_x):
                for j in range(NJ):
                    ins = dve.tensor_scalar(xo[:, j, :], h[:, j, :], mv[:, j, 0:1], rs[:, j:j + 1], ALU.subtract, ALU.mult)
                ins.then_inc(s_x, 1)

            def group(g):
                if live(g - 1):
                    dve.wait_ge(s_rs3, g)
                    normal(h3, mv3, rs3, x3, s_x3)
                if live(g):
                    dve.wait_ge(s_s3, g + 1)
                    dve.scalar_tensor_tensor(out=sm[:, :, :], in0=PS[:, 2, :].rearrange("p (j n) -> p j n", j=NJ), scalar=float(D) ** -0.5,
                                             in1=blockmask[:, None, :].to_broadcast([P, NJ, P]), op0=ALU.mult, op1=ALU.add).then_inc(s_sm, 1)
                    dve.wait_ge(s_sm, 2 * g + 1)
                    dve.tensor_reduce(nm3[:, :], sm[:, :, :], AX.X, ALU.max, negate=True).then_inc(s_sm, 1)
                if live(g + 1):
                    combine(1, g + 1)
                    dve.wait_ge(s_comb, T + g + 2)
                    stats(lambda b: x1_all[:, bass.ds(b * T + g + 1, 1), :].rearrange("p o d -> p (o d)"), st2, mv2, ve2, s_var2)
                if live(g - 2):
                    dve.wait_ge(s_f2, g - 1)
                    if after_first(g - 2):
                        dve.wait_ge(s_x4, g - 2)
                    dve.tensor_tensor(h4[:, :, :], PS[:, 7, :].rearrange("p (j d) -> p j d", j=NJ), x3b[:, :, :], ALU.add).then_inc(s_h4, 1)
                    dve.wait_ge(s_h4, g - 1)
                    stats(lambda j: h4[:, j, :], st4, mv4, ve4, s_var4)
                if live(g - 1):
                    dve.wait_ge(s_x3, g)
                    dve.tensor_tensor(x3b[:, :, :], x3[:, :, :], b2_s[:, None, :].to_broadcast([P, NJ, D]), ALU.add).then_inc(s_x3b, 1)
                if live(g + 1):
                    dve.wait_ge(s_rs2, g + 2)
                    dve.scalar_tensor_tensor(out=nb2[:, :], in0=mv2[:, :, 0], scalar=-1.0, in1=rs2[:, :], op0=ALU.mult, op1=ALU.mult).then_inc(s_nb2, 1)
                if live(g):
                    dve.wait_ge(s_p3, NJ * (g + 1))
                    own.add(dve.reciprocal(inv3[:, :], sum3[:, :]))
                    own.wait()
                    dve.wait_ge(s_pv3, g + 1)
                    for j in range(NJ):
                        ins = dve.scalar_tensor_tensor(out=h3[:, j, :], in0=PS[:, 4, j * D:(j + 1) * D], scalar=inv3[:, j:j + 1],
                                                       in1=xv[:, j, :], op0=ALU.mult, op1=ALU.add)
                    ins.then_inc(s_h3, 1)
                    dve.wait_ge(s_h3, g + 1)
                    stats(lambda j: h3[:, j, :], st3, mv3, ve3, s_var3)
                if live(g - 2):
                    dve.wait_ge(s_rs4, g - 1)
                    if after_first(g - 2):
                        dve.wait_ge(s_out, 16 * B * (g - 2))
                    normal(h4, mv4, rs4, x4, s_x4)
                own.close()

            for g in range(-1, 2):
                group(g)
            with dve.Fori(2, T - 1) as g:
                group(g)
            for g in range(T - 1, T + 2):
                group(g)

        @block.tensor
        def _(pe):
            def k_mm(b):
                pe.wait_ge(s_xT, 16 * (b + 1))
                for h in range(2):
                    mm = pe.matmul(PS[:, h, :], wkT_s[:, :], xT_s[:, h * 512:(h + 1) * 512], start=True, stop=True)
                mm.then_inc(s_k_mm, 1)

            def q_mm(b):
                for h in range(2):
                    mm = pe.matmul(PS[:, 2 + h, :], wqT_s[:, :], xT_s[:, h * 512:(h + 1) * 512], start=True, stop=True)
                mm.then_inc(s_q_mm, 1)

            def v_mm(b):
                for h in range(2):
                    for t in range(4):
                        mm = pe.matmul(PS[:, 4 + h, t * D:(t + 1) * D], xT_s[:, (4 * h + t) * P:(4 * h + t + 1) * P], wvoT_s[:, :],
                                       start=True, stop=True)
                    mm.then_inc(s_v_mm, 1)

            def scores(g, t):
                for h in range(2):
                    mm = pe.matmul(PS[:, 2 * (t % 2) + h, :], QT[:, t * P:(t + 1) * P], KT[:, h * 512:(h + 1) * 512], start=True, stop=True)
                mm.then_inc(s_s, 1)

            def turn(src, cols, bank, n):
                for i in range(n):
                    mm = pe.transpose(PS[:, bank, i * P:(i + 1) * P], cols(i) if src is None else src[:, i, :], ident)
                return mm

            def router_turn(r, h):
                if h == 0:
                    pe.wait_ge(s_x1, r + 1)
                if not isinstance(r, int) or r or h:
                    pe.wait_ge(s_r_ev, 4 * r + h)
                else:
                    pe.wait_ge(s_prep_ev, 4)
                for t in range(4):
                    mm = pe.transpose(PS[:, 7, t * P:(t + 1) * P], x1b[:, 4 * h + t, :], ident)
                mm.then_inc(s_r_mm, 1)

            def router_logits(r):
                pe.wait_ge(s_r_ev, 4 * r + 2)
                for t in range(T):
                    mm = pe.matmul(PS[:, 7, t * E:(t + 1) * E], x1T[:, t * P:(t + 1) * P], gateT_s[:, :], start=True, stop=True)
                mm.then_inc(s_r_mm, 1)

            def router_count(r, bank=7):
                pe.wait_ge(s_both, r + 1)
                pe.matmul(PS[:, bank, 0:T * E], tri, both[:, :, :].rearrange("p t e -> p (t e)"), start=True, stop=False)
                pe.matmul(PS[:, bank, 0:T * E], ones, before[:, :, :].rearrange("p t e -> p (t e)"), start=False, stop=True).then_inc(s_r_mm, 1)

            def body(b, first=False, last=False):
                for t in range(T):
                    g = b * T + t
                    pe.wait_ge(s_exp, g + 1)
                    for h, ev in ((0, s_e0), (1, s_e1)):
                        if not (first and t == 0):
                            pe.wait_ge(ev, g)
                        if t == 0:
                            pe.wait_ge((s_v0_ev, s_v1_ev)[h], b + 1)
                        for k in range(4):
                            mm = pe.transpose(PS[:, 4 + h, k * P:(k + 1) * P], prob[:, t % 2, (4 * h + k) * P:(4 * h + k + 1) * P], ident)
                        mm.then_inc(s_t, 1)
                    if t == 1 and not first:
                        router_turn(b - 1, 1)
                    if t == 7 and not last:
                        q_mm(b + 1)
                    if t + 2 < T:
                        scores(g + 2, t + 2)
                    if t == 4 and not first:
                        router_count(b - 1)
                    pe.wait_ge(s_e0, g + 1)
                    pe.wait_ge(s_e1, g + 1)
                    if not (first and t == 0):
                        pe.wait_ge(s_o, g)
                    for k in range(T):
                        mm = pe.matmul(PS[:, 6, 0:D], PT[:, k, :], V[:, k, :], start=(k == 0), stop=(k == T - 1))
                    mm.then_inc(s_pv, 1)
                    if t == 0 and not first:
                        router_turn(b - 1, 0)
                    if t == 1 and not first:
                        router_logits(b - 1)
                    if t == 6 and not last:
                        k_mm(b + 1)
                if not last:
                    v_mm(b + 1)
                    pe.wait_ge(s_k_ev, b + 2)
                    pe.wait_ge(s_q_ev, b + 2)
                    scores(b * T + T, 0)
                    scores(b * T + T + 1, 1)

            pe.wait_ge(s_ld0, 16 * 13)
            k_mm(0)
            q_mm(0)
            pe.matmul(PS[:, 6, 0:D], wv_s[:, :], woT_s[:, :], start=True, stop=True).then_inc(s_prep_mm, 1)
            pe.wait_ge(s_bvw, 1)
            pe.matmul(PS[:, 7, 0:D], bv_wide[:, :], woT_s[:, :], start=True, stop=True).then_inc(s_prep_mm, 1)
            pe.wait_ge(s_prep_ev, 1)
            v_mm(0)
            pe.wait_ge(s_k_ev, 1)
            pe.wait_ge(s_q_ev, 1)
            scores(0, 0)
            scores(1, 1)
            pe.wait_ge(s_ld1, 64)
            pe.wait_ge(s_prep_ev, 2)
            pe.matmul(PS[:, 6, :], u1T_s[:, :], v1_s[:, :], start=True, stop=True).then_inc(s_prep_mm, 1)
            for c in range(FC):
                mm = pe.matmul(PS[:, 7, c * D:(c + 1) * D], u2T_s[:, c * P:(c + 1) * P], v2_s[:, :], start=True, stop=True)
            mm.then_inc(s_prep_mm, 1)
            pe.wait_ge(s_prep_ev, 4)
            body(0, first=True)
            with pe.Fori(1, B - 1) as b:
                body(b)
            body(B - 1, last=True)
            def slots_T(j, u, n):
                pe.wait_ge(s_Xn[u], 16 * (n + 1))
                for q in range(Q):
                    mm = pe.transpose(PS[:, q // 4, (q % 4) * P:(q % 4 + 1) * P], Xn[:, u, q * D:(q + 1) * D], ident)
                mm.then_inc(s_XT_mm, 1)

            def unit(j, u, k, n, first=False):
                if k == 0:
                    pe.wait_ge(s_XTl, j + 1)
                    pe.wait_ge(s_wl, j + 1)
                if not first:
                    pe.wait_ge(s_g, NU * j + k - 1)
                c, h = k // 2, k % 2
                cols = slice(h * HALF, (h + 1) * HALF)
                xh, xl = XTh[:, u, cols], XTl[:, u, cols]

                def product(bank, chunk):
                    w = slice(chunk * P, (chunk + 1) * P)
                    pe.matmul(PS[:, bank, 0:HALF], w13h[:, u, w], xh, start=True, stop=False)
                    pe.matmul(PS[:, bank, 0:HALF], w13h[:, u, w], xl, start=False, stop=False)
                    return pe.matmul(PS[:, bank, 0:HALF], w13l[:, u, w], xh, start=False, stop=True)

                bank = 2 + 2 * (k % 2)
                product(bank, c).then_inc(s_ha, 1)
                if c < 3:
                    product(bank + 1, 4 + c).then_inc(s_h, 1)

            def down(j, u, n, first=False):
                pe.wait_ge(s_w[u], 32 * (n + 1))
                pe.wait_ge(s_g, NU * (j + 1))
                if not first:
                    pe.wait_ge(s_ye, j)
                for q in range(Q):
                    for c in range(4):
                        n = P if c < 3 else FT
                        mm = pe.matmul(PS[:, 6 + q // 4, (q % 4) * D:(q % 4 + 1) * D], G[0:n, u, c, q * P:(q + 1) * P], w2_s[0:n, u, c, :],
                                       start=(c == 0), stop=(c == 3))
                mm.then_inc(s_y, 1)

            def pass_(j, u, n, first=False, between=lambda k: None):
                m = n + (1 if u else 0)
                for k in range(2, NU):
                    if k == 6 and live(j + 1, J):
                        slots_T(j + 1, 1 - u, m)
                    unit(j, u, k, n)
                    between(k)
                if live(j + 1, J):
                    unit(j + 1, 1 - u, 0, m)
                    unit(j + 1, 1 - u, 1, m)
                if first:
                    router_logits(B - 1)
                    pe.wait_ge(s_r_ev, 4 * B - 1)
                down(j, u, n, first)

            def router_parts(k):
                if k in (5, 7):
                    router_turn(B - 1, (k - 5) // 2)

            slots_T(0, 0, 0)
            unit(0, 0, 0, 0, first=True)
            unit(0, 0, 1, 0, first=True)
            pass_(0, 0, 0, first=True, between=router_parts)
            pass_(1, 1, 0)
            router_count(B - 1, bank=1)
            pe.wait_ge(s_r_ev, 4 * B)
            with pe.Fori(1, J // 2 - 1) as i:
                pass_(2 * i, 0, i)
                pass_(2 * i + 1, 1, i)
            pass_(J - 2, 0, J // 2 - 1)
            pass_(J - 1, 1, J // 2 - 1)

            def ffn_up(g, c):
                if c == 0:
                    pe.wait_ge(s_x3T_ev, g + 1)
                if c >= 2:
                    pe.wait_ge(s_gelu, FC * g + c - 1)
                pe.matmul(PS[:, 5 + c % 2, :], f1_s[:, c * P:(c + 1) * P], x3T[:, :], start=True, stop=True).then_inc(s_f1, 1)

            def ffn_down(g):
                pe.wait_ge(s_gelu, FC * g + FC)
                if after_first(g):
                    pe.wait_ge(s_h4, g)
                for j in range(NJ):
                    for c in range(FC):
                        mm = pe.matmul(PS[:, 7, j * D:(j + 1) * D], H[:, c, j * P:(j + 1) * P], f2_s[:, c, :], start=(c == 0), stop=(c == FC - 1))
                mm.then_inc(s_f2, 1)

            def group(g):
                if live(g):
                    pe.wait_ge(s_x2T_ev, g + 1)
                    for j in range(NJ):
                        mm = pe.transpose(PS[:, 1, j * P:(j + 1) * P], x2T[:, j, :], ident)
                    mm.then_inc(s_xv_mm, 1)
                    for j in range(NJ):
                        mm = pe.matmul(PS[:, 2, j * P:(j + 1) * P], x2T[:, j, :], x2T[:, j, :], start=True, stop=True)
                    mm.then_inc(s_s3, 1)
                if live(g - 2):
                    ffn_down(g - 2)
                if live(g):
                    pe.wait_ge(s_p3, NJ * (g + 1))
                    for j in range(NJ):
                        mm = pe.transpose(PS[:, 3, j * P:(j + 1) * P], p3[:, j, :], ident)
                    mm.then_inc(s_p3T_mm, 1)
                if live(g - 1):
                    pe.wait_ge(s_x3, g)
                    for j in range(NJ):
                        mm = pe.transpose(PS[:, 0, j * P:(j + 1) * P], x3[:, j, :], ident)
                    mm.then_inc(s_x3T_mm, 1)
                    ffn_up(g - 1, 0)
                    ffn_up(g - 1, 1)
                if live(g):
                    pe.wait_ge(s_p3T_ev, g + 1)
                    pe.wait_ge(s_xv_ev, g + 1)
                    for j in range(NJ):
                        mm = pe.matmul(PS[:, 4, j * D:(j + 1) * D], p3T[:, j, :], xv[:, j, :], start=True, stop=True)
                    mm.then_inc(s_pv3, 1)
                if live(g - 1):
                    ffn_up(g - 1, 2)
                    ffn_up(g - 1, 3)
                if live(g + 1):
                    pe.wait_ge(s_x2, g + 2)
                    for b in range(B):
                        mm = pe.transpose(PS[:, 0, b * P:(b + 1) * P], x2[:, b, :], ident)
                    mm.then_inc(s_x2T_mm, 1)

            for g in range(-1, 2):
                group(g)
            with pe.Fori(2, T - 1) as g:
                group(g)
            for g in range(T - 1, T + 2):
                group(g)


def tables():
    c = np.zeros((P, C_END), np.float32)
    i = np.arange(P)
    c[:, C_ID:C_ID + P] = np.eye(P)
    c[:, C_TRI:C_TRI + P] = i[:, None] <= i[None, :]
    c[:, C_ONE:C_ONE + P] = 1
    c[:, C_BLK:C_BLK + P] = np.where(i[:, None] % SUB == i[None, :] % SUB, 0.0, -1e30)
    b, k, t = np.meshgrid(np.arange(B), np.arange(K), np.arange(T), indexing="ij")
    c[:, C_BASE:C_TRASH] = ((b // 2) * E * SLOTS + (b % 2) * CAP - 1).reshape(1, -1)
    c[:, C_TRASH:C_IOTA] = ROWS + ((b * K + k) * T + t).reshape(1, -1) * P + i[:, None]
    c[:, C_IOTA:C_END] = np.arange(E)
    s = np.arange(S, dtype=np.float32)
    g = np.exp(np.float32(-0.5) * ((s - np.float32(S / 2)) / np.float32(S / 4)) ** 2) / np.sqrt(np.float32(D))
    return c, np.ascontiguousarray(np.broadcast_to(g.astype(np.float32)[None, :], (P, S)))


def kernel(**inputs):
    import concourse.bacc as _bacc
    from concourse.bass_utils import run_bass_kernel_spmd as _run

    def a(name):
        return np.asarray(inputs[name])

    consts, gmask = tables()
    x = a("L0_attn_x").reshape(B * S, D)
    w1, w3 = a("L0_ffn_w1"), a("L0_ffn_w3")
    laid = {
        "xT": x.T, "x": x,
        "wqT": a("L0_attn_Wq").T, "wkT": a("L0_attn_Wk").T, "wv": a("L0_attn_Wv"), "woT": a("L0_attn_Wo").T,
        "bq": a("L0_attn_bq").reshape(D, 1), "bk": a("L0_attn_bk").reshape(D, 1), "bv": a("L0_attn_bv").reshape(D, 1),
        "bo": np.broadcast_to(a("L0_attn_bo").reshape(1, D), (P, D)),
        "gateT": a("L0_ffn_gate_w").T,
        "w13": np.concatenate([w1, w3[:, :, 3 * P:], w3[:, :, :3 * P]], axis=2),
        "w2": a("L0_ffn_w2"),
        "u1T": a("L1_ffn_U1").T, "v1": a("L1_ffn_V1"), "u2T": a("L1_ffn_U2").T, "v2": a("L1_ffn_V2"),
        "b1": a("L1_ffn_b1").reshape(FC, P).T, "b2": np.broadcast_to(a("L1_ffn_b2").reshape(1, D), (P, D)),
        "consts": consts, "gmask": gmask,
    }
    nc = _bacc.Bacc("TRN2", target_bir_lowering=False, num_devices=1)
    arrays, args = {}, []
    for name, v in laid.items():
        v = np.ascontiguousarray(v)
        arrays[f"in_{name}"] = v
        args.append(nc.dram_tensor(f"in_{name}", v.shape, mybir.dt.from_np(v.dtype), kind="ExternalInput").ap())
    args.append(nc.dram_tensor("out_0", (B, S, D), F32, kind="ExternalOutput").ap())
    build(nc, *args)
    r = _run(nc, [arrays], core_ids=[0])
    return r.results[0]["out_0"]
```

```python
from contextlib import ExitStack

import numpy as np

import concourse.bass as bass
from concourse import mybir

F32 = mybir.dt.float32
F32R = mybir.dt.float32r
U32 = mybir.dt.uint32
ALU = mybir.AluOpType
ACT = mybir.ActivationFunctionType
AX = mybir.AxisListType

P = 128
B, S, D = 4, 1024, 128
E, K, F = 8, 2, 448
CAP = int(S * K / E * 1.25)
DFF, RANK = 512, 32
EPS = 1e-5
T = S // P
NT = B * T
PAIRS = B // 2
SLOTS = 2 * CAP
Q = SLOTS // P
J = PAIRS * E
ROWS = J * SLOTS
FT = F - 3 * P
HALF = SLOTS // 2
NU = 8
SUB = 32
NJ = P // SUB
FC = DFF // P
FAR = -32768.0
HIDDEN_BANKS = (5, 6, 2, 1)
EARLY = 2

C_ID, C_TRI, C_ONE, C_BLK = 0, P, 2 * P, 3 * P
C_BASE = 4 * P
C_TRASH = C_BASE + B * K * T
C_IOTA = C_TRASH + B * K * T
C_END = C_IOTA + E


class Steps:

    def __init__(self, eng, sem):
        self.eng, self.sem, self.n = eng, sem, 0

    def add(self, ins):
        ins.then_inc(self.sem, 1)
        self.n += 1

    def wait(self, back=0):
        self.eng.wait_ge(self.sem, self.n - back)

    def close(self):
        self.wait()
        self.eng.sem_clear(self.sem)
        self.n = 0


def live(n, count=T):
    return not isinstance(n, int) or 0 <= n < count


def after_first(n):
    return not isinstance(n, int) or n > 0


ORDER = (0, 1, 2, 6, 3, 4, 7, 5)
FULL = tuple(sum(o < 6 for o in ORDER[:k + 1]) for k in range(len(ORDER)))


def unit_bank(k):
    return (2, 4, 0)[k % 3]


def build(nc, xT, x, wqT, wkT, wv, woT, bq, bk, bv, bo, gateT, w13, w2, u1T, v1, u2T, v2, b1, b2, consts, gmask, out):
    ctx = ExitStack()
    with ctx:
        def sb(name, shape, dt=F32):
            return ctx.enter_context(nc.sbuf_tensor(name, shape, dt))

        def sem(name):
            return ctx.enter_context(nc.semaphore(name))

        x_slots = nc.dram_tensor("x_slots", (ROWS + NT * P * K, D), F32, kind="Internal").ap()
        y_slots = nc.dram_tensor("y_slots", (ROWS, D), F32, kind="Internal").ap()

        cst = sb("cst", [P, C_END])
        ident, tri, ones = cst[:, C_ID:C_ID + P], cst[:, C_TRI:C_TRI + P], cst[:, C_ONE:C_ONE + P]
        blockmask = cst[:, C_BLK:C_BLK + P]
        base_tab = cst[:, C_BASE:C_TRASH].rearrange("p (b n) -> p b n", b=B)
        trash_tab = cst[:, C_TRASH:C_IOTA].rearrange("p (b n) -> p b n", b=B)
        iota = cst[:, C_IOTA:C_END]
        gm = sb("gm", [P, S])
        wqT_s, wkT_s, wv_s, woT_s = (sb(n, [P, D]) for n in ("wqT_s", "wkT_s", "wv_s", "woT_s"))
        wvoT_s = sb("wvoT_s", [P, D])
        bq_s, bk_s, bv_s = sb("bq_s", [P, 1]), sb("bk_s", [P, 1]), sb("bv_s", [P, 1])
        bv_wide = sb("bv_wide", [P, P])
        bo_s, beff = sb("bo_s", [P, D]), sb("beff", [P, D])
        gateT_s = sb("gateT_s", [P, E])
        u1T_s, v1_s = sb("u1T_s", [RANK, D]), sb("v1_s", [RANK, DFF])
        u2T_s, v2_s = sb("u2T_s", [RANK, DFF]), sb("v2_s", [RANK, D])
        f1_s, f2_s = sb("f1_s", [P, DFF]), sb("f2_s", [P, FC, D])
        b1_s, b2_s = sb("b1_s", [P, FC]), sb("b2_s", [P, D])
        zeros = sb("zeros", [P, 2560])
        warm = sb("warm", [P, 1])
        mhalf = sb("mhalf", [P, T])

        xT_s, xn_s, xb_s = sb("xT_s", [P, S]), sb("xn_s", [P, T, D]), sb("xb_s", [P, T, D])
        KT, V = sb("KT", [P, S]), sb("V", [P, T, D])
        QTh, QTl, KTh, KTl = (sb(n, [P, S], F32R) for n in ("QTh", "QTl", "KTh", "KTl"))
        prob = sb("prob", [P, 2, S])
        PT = sb("PT", [P, T, P])
        nmax, rsum, rinv = sb("nmax", [P, T]), sb("rsum", [P, T]), sb("rinv", [P, T])
        h1 = sb("h1", [P, T, D])
        st1, mv1 = sb("st1", [P, T, 6]), sb("mv1", [P, T, 2])
        ve1, rs1 = sb("ve1", [P, T]), sb("rs1", [P, T])
        x1b = sb("x1b", [P, T, D])
        x1_all = sb("x1_all", [P, NT, D])
        x1T = sb("x1T", [P, S])
        lg, lmx, lsh, lex = sb("lg", [P, T, E]), sb("lmx", [P, T]), sb("lsh", [P, T, E]), sb("lex", [P, T, E])
        lsum, linv, pr = sb("lsum", [P, T]), sb("linv", [P, T]), sb("pr", [P, T, E])
        top, tix = sb("top", [P, T, E]), sb("tix", [P, T, E], U32)
        tixf = sb("tixf", [P, K, T])
        oh = sb("oh", [P, K, T, E])
        both = sb("both", [P, T + 4, E])
        upto = sb("upto", [P, 2, T + 4, E])
        cnt = sb("cnt", [P, T, E])
        ohc = sb("ohc", [P, K, T, E])
        pos = sb("pos", [P, K * T])
        row_g, row_d = sb("row_g", [P, K * T]), sb("row_d", [P, K * T])
        row_s, row_t = sb("row_s", [P, K * T]), sb("row_t", [P, K * T])
        sidx = sb("sidx", [P, K * T], U32)
        gidx = sb("gidx", [P, B, K * T], U32)
        wts = sb("wts", [P, B, K * T])
        Xn = sb("Xn", [P, 2, Q * D])
        XTh, XTl = sb("XTh", [P, 2, SLOTS], F32R), sb("XTl", [P, 2, SLOTS], F32R)
        w13_s = sb("w13_s", [P, 2, 2 * F])
        w13h, w13l = sb("w13h", [P, 2, 2 * F], F32R), sb("w13l", [P, 2, 2 * F], F32R)
        xTh, xTl = (t[:, :, :].rearrange("p u n -> p (u n)")[:, 0:S] for t in (XTh, XTl))
        wkh, wqh, wkl, wql = (t[:, 0, i * D:(i + 1) * D] for t in (w13h, w13l) for i in range(2))
        w2_s = sb("w2_s", [P, 2, 4, D])
        sil = sb("sil", [P, 3, HALF])
        G = sb("G", [P, 2, 4, SLOTS])
        Ys = sb("Ys", [P, 2, Q * D])
        gi_s, wt_s = sb("gi_s", [P, 2 * K], U32), sb("wt_s", [P, 2 * K])
        GA = sb("GA", [P, 2 * K, D])
        gi0_s, wt0_s, GA0 = sb("gi0_s", [P, 2 * K], U32), sb("wt0_s", [P, 2 * K]), sb("GA0", [P, 2 * K, D])
        x2 = sb("x2", [P, B, D])
        st2, mv2, ve2, rs2 = sb("st2", [P, B, 6]), sb("mv2", [P, B, 2]), sb("ve2", [P, B]), sb("rs2", [P, B])
        x2T = sb("x2T", [P, NJ, B * SUB])
        xv = sb("xv", [P, NJ, D + 1])
        inv3 = sb("inv3", [P, NJ])
        p3 = sb("p3", [P, NJ, P])
        far, far_ident = KTh[:, 0:NJ * P], KTl[:, 0:P]
        h3 = sb("h3", [P, NJ, D])
        st3, mv3, ve3, rs3 = sb("st3", [P, NJ, 6]), sb("mv3", [P, NJ, 2]), sb("ve3", [P, NJ]), sb("rs3", [P, NJ])
        x3, x3b = sb("x3", [P, NJ, D]), sb("x3b", [P, 2, NJ, D])
        x3Th, x3Tl = QTh[:, 0:NJ * P], QTl[:, 0:NJ * P]
        f1h, f1l = QTh[:, NJ * P:NJ * P + DFF], QTl[:, NJ * P:NJ * P + DFF]
        H = prob[:, :, :].rearrange("p h (c n) -> p (h c) n", n=NJ * P)
        h4 = sb("h4", [P, NJ, D])
        st4, mv4, ve4, rs4 = sb("st4", [P, NJ, 6]), sb("mv4", [P, NJ, 2]), sb("ve4", [P, NJ]), sb("rs4", [P, NJ])
        x4 = xn_s[:, 0:NJ, :]
        mr4, nb4 = sb("mr4", [P, 2]), sb("nb4", [P, 2])

        PS = ctx.enter_context(nc.psum_tensor("PS", [P, 8, 512], F32))

        s_ldw = sem("s_ldw")
        s_ldb = sem("s_ldb")
        s_ldv = sem("s_ldv")
        s_ld0 = sem("s_ld0")
        s_ld1 = sem("s_ld1")
        s_xT = sem("s_xT")
        s_xn = sem("s_xn")
        s_zero = sem("s_zero")
        s_x1all = sem("s_x1all")
        s_Xn = [sem("s_Xn0"), sem("s_Xn1")]
        s_w13 = [sem("s_w130"), sem("s_w131")]
        s_w = [sem("s_w0"), sem("s_w1")]
        s_yst = [sem("s_yst0"), sem("s_yst1")]
        s_out = sem("s_out")
        s_init = sem("s_init")
        s_xb = sem("s_xb")
        s_rs1 = sem("s_rs1")
        s_sc = sem("s_sc")
        s_pool = sem("s_pool")
        s_ga = sem("s_ga")
        s_ga0 = sem("s_ga0")
        s_rs2, s_rs3, s_rs4 = sem("s_rs2"), sem("s_rs3"), sem("s_rs4")
        s_prep_mm = sem("s_prep_mm")
        s_prep_ev = sem("s_prep_ev")
        s_bvw = sem("s_bvw")
        s_k_mm, s_q_mm, s_v_mm = sem("s_k_mm"), sem("s_q_mm"), sem("s_v_mm")
        s_kqh, s_kql = sem("s_kqh"), sem("s_kql")
        s_xh, s_xl = sem("s_xh"), sem("s_xl")
        s_k_ev = sem("s_k_ev")
        s_kh, s_kl = sem("s_kh"), sem("s_kl")
        s_qh, s_ql = sem("s_qh"), sem("s_ql")
        s_v_ev = sem("s_v_ev")
        s_s = sem("s_s")
        s_max = sem("s_max")
        s_exp = sem("s_exp")
        s_t = sem("s_t")
        s_e = sem("s_e")
        s_pv = sem("s_pv")
        s_o = sem("s_o")
        s_own = sem("s_own")
        s_var1 = sem("s_var1")
        s_x1 = sem("s_x1")
        s_r_mm = sem("s_r_mm")
        s_r_ev = sem("s_r_ev")
        s_lsh = sem("s_lsh")
        s_lex = sem("s_lex")
        s_both = sem("s_both")
        s_idx = sem("s_idx")
        s_XT_mm = sem("s_XT_mm")
        s_XTh, s_XTl = sem("s_XTh"), sem("s_XTl")
        s_wh, s_wl = sem("s_wh"), sem("s_wl")
        s_ha = sem("s_ha")
        s_h = sem("s_h")
        s_sil = sem("s_sil")
        s_g = sem("s_g")
        s_y = sem("s_y")
        s_ye, s_ye1 = sem("s_ye"), sem("s_ye1")
        s_comb = sem("s_comb")
        s_var2, s_var3, s_var4 = sem("s_var2"), sem("s_var3"), sem("s_var4")
        s_x2 = sem("s_x2")
        s_x2T_mm, s_x2T_ev = sem("s_x2T_mm"), sem("s_x2T_ev")
        s_xv_mm, s_xv_ev = sem("s_xv_mm"), sem("s_xv_ev")
        s_s3 = sem("s_s3")
        s_p3 = sem("s_p3")
        s_far = sem("s_far")
        s_pv3 = sem("s_pv3")
        s_h3 = sem("s_h3")
        s_x3 = sem("s_x3")
        s_x3b = sem("s_x3b")
        s_x3T_mm = sem("s_x3T_mm")
        s_x3Th, s_x3Tl = sem("s_x3Th"), sem("s_x3Tl")
        s_f1h, s_f1l = sem("s_f1h"), sem("s_f1l")
        s_f1 = sem("s_f1")
        s_gelu = sem("s_gelu")
        s_f2 = sem("s_f2")
        s_h4 = sem("s_h4")
        s_var2h, s_rs2h, s_x2h = (sem(n) for n in ("s_var2h", "s_rs2h", "s_x2h"))
        s_nb4 = sem("s_nb4")
        s_x4, s_x4b = sem("s_x4"), sem("s_x4b")
        s_f2h, s_h4h, s_var4h, s_rs4h, s_x4h = (sem(n) for n in ("s_f2h", "s_h4h", "s_var4h", "s_rs4h", "s_x4h"))

        block = ctx.enter_context(nc.Block())

        @block.sync
        def _(sp):
            def load(dst, src, s):
                sp.dma_start(dst, src).then_inc(s, 16)

            load(xT_s[:, :], xT[:, 0:S], s_xT)
            load(wkT_s[:, :], wkT, s_ldw)
            load(wqT_s[:, :], wqT, s_ldw)
            load(wv_s[:, :], wv, s_ldv)
            load(woT_s[:, :], woT, s_ldv)
            load(bv_s[:, :], bv, s_ldv)
            load(bo_s[:, :], bo, s_ldv)
            load(cst[:, :], consts, s_ld0)
            load(xn_s[:, :, :], x[0:S, :].rearrange("(t p) d -> p t d", p=P), s_xn)
            load(gateT_s[:, :], gateT, s_ld0)
            load(b1_s[:, :], b1, s_ld0)
            load(b2_s[:, :], b2, s_ld0)
            load(u1T_s[:, :], u1T, s_ld1)
            load(v1_s[:, :], v1, s_ld1)
            load(u2T_s[:, :], u2T, s_ld1)
            load(v2_s[:, :], v2, s_ld1)
            sp.wait_ge(s_init, 2)
            zr = x_slots[0:ROWS, :].rearrange("(q p t) d -> q p (t d)", p=P, t=2560 // D)
            for q in range(zr.shape[0]):
                load(zr[q], zeros[:, :], s_zero)

            def up_weights(j, u):
                load(w13_s[:, u, :], w13[bass.ds(j % E, 1), :, :].rearrange("e p n -> p (e n)"), s_w13[u])

            def down_weights(j, u):
                load(w2_s[:, u, 0:3, :], w2[bass.ds(j % E, 1), 0:3 * P, :].rearrange("e (c p) d -> p (e c) d", p=P), s_w[u])
                load(w2_s[0:FT, u, 3, :], w2[bass.ds(j % E, 1), 3 * P:F, :].rearrange("e p d -> p (e d)"), s_w[u])

            with sp.Fori(0, B - 1) as b:
                sp.wait_ge(s_v_mm, 2 * b + 2)
                load(xT_s[:, :], xT[:, bass.ds((b + 1) * S, S)], s_xT)
                sp.wait_ge(s_xb, b + 1)
                load(xn_s[:, :, :], x[bass.ds((b + 1) * S, S), :].rearrange("(t p) d -> p t d", p=P), s_xn)
                sp.wait_ge(s_x1, b + 1)
                load(x1_all[:, bass.ds(b * T, T), :], x1b[:, :, :], s_x1all)
            for j in range(2):
                up_weights(j, j)
                down_weights(j, j)

            def slots_in(j, u):
                load(Xn[:, u, :], x_slots[bass.ds(j * SLOTS, SLOTS), :].rearrange("(p t) d -> p (t d)", p=P), s_Xn[u])

            def slots_out(j, u):
                sp.wait_ge(s_ye, j + 1)
                sp.wait_ge(s_ye1, j + 1)
                load(y_slots[bass.ds(j * SLOTS, SLOTS), :].rearrange("(p t) d -> p (t d)", p=P), Ys[:, u, :], s_yst[u])

            slots_in(0, 0)
            slots_in(1, 1)
            def operands(j, u, i):
                if live(j, J):
                    sp.wait_ge(s_wl, j - 1)
                    up_weights(j, u)
                    sp.wait_ge(s_XT_mm, j - 1)
                    if u == 0:
                        sp.wait_ge(s_sc, 16 * K * T * (B // 2 + B // 2 * ((i + 2) // (J // 4))))
                    slots_in(j, u)

            def pass_(i, u):
                j = 2 * i + u
                operands(j + 3, 1 - u, min(i, J // 2 - 3) if isinstance(i, int) else i)
                sp.wait_ge(s_y, j + 1)
                down_weights(j + 2, u)
                slots_out(j, u)

            operands(2, 0, -1)
            sp.wait_ge(s_x1, B)
            load(x1_all[:, (B - 1) * T:NT, :], x1b[:, :, :], s_x1all)
            with sp.Fori(0, J // 2 - 2) as i:
                pass_(i, 0)
                pass_(i, 1)
            pass_(J // 2 - 2, 0)
            pass_(J // 2 - 2, 1)
            slots_out(J - 2, 0)
            slots_out(J - 1, 1)

            def store(g):
                for b in range(B):
                    load(out[b, bass.ds(g * P, P), :].rearrange("(j s) d -> s j d", s=SUB),
                         x4[b * SUB:(b + 1) * SUB, :, :], s_out)

            with sp.Fori(0, T - 1) as g:
                sp.wait_ge(s_x4, g + 1)
                sp.wait_ge(s_x4b, g + 1)
                store(g)
            sp.wait_ge(s_x4h, 2)
            store(T - 1)
            sp.wait_ge(s_out, 16 * B * T)

        @block.gpsimd
        def _(pool):
            own = Steps(pool, s_pool)
            pool.memset(zeros[:, 0:1], 0.0).then_inc(s_init, 1)
            pool.memset(zeros[:, 1:], 0.0).then_inc(s_init, 1)
            pool.memset(mhalf[:, :], -0.5).then_inc(s_init, 1)
            pool.memset(xv[:, :, D:D + 1], 1.0).then_inc(s_init, 1)
            pool.memset(both[:, 0:4, :], 0.0).then_inc(s_init, 1)
            pool.memset(upto[:, :, 0:4, :], 0.0).then_inc(s_init, 1)

            def x_plus_bias(b):
                if not isinstance(b, int) or b > 0:
                    pool.wait_ge(s_o, T * b)
                else:
                    pool.wait_ge(s_prep_ev, 2)
                pool.wait_ge(s_xn, 16 * b + 16)
                pool.tensor_tensor(xb_s[:, :, :], xn_s[:, :, :], beff[:, None, :].to_broadcast([P, T, D]),
                                   ALU.add).then_inc(s_xb, 1)

            def scatter(r):
                pool.wait_ge(s_zero, 16 * (ROWS * D // (P * 2560)))
                pool.wait_ge(s_idx, r + 1)
                pool.engine_nop()
                for k in range(K):
                    for t in range(T):
                        pool.indirect_dma_start(x_slots[:, :], bass.IndirectOffsetOnAxis(ap=sidx[:, k * T + t:k * T + t + 1], axis=0),
                                                x1b[:, t, :], None).then_inc(s_sc, 16)

            def rstd1(b):
                pool.wait_ge(s_var1, b + 1)
                pool.tensor_tensor(rs1[:, :], ve1[:, :], mhalf[:, :], ALU.pow).then_inc(s_rs1, 1)

            pool.wait_ge(s_init, 6)
            x_plus_bias(0)
            rstd1(0)
            with pool.Fori(1, B) as b:
                x_plus_bias(b)
                scatter(b - 1)
                rstd1(b)
            scatter(B - 1)

            def gather_indices(pair, g, gi, wt):
                for src, dst in ((gidx, gi), (wts, wt)):
                    own.add(pool.tensor_copy(dst[:, :], src[:, 2 * pair:2 * pair + 2, :].rearrange("p b (k t) -> p (b k) t", k=K)[:, :, g]))
                own.close()

            def gather_rows(pair, i, gi=gi_s, rows=GA, s=s_ga):
                pool.indirect_dma_start(rows[:, i, :], None, y_slots[0:(pair + 1) * E * SLOTS, :],
                                        bass.IndirectOffsetOnAxis(ap=gi[:, i:i + 1], axis=0)).then_inc(s, 16)

            def rstd(n, var, s_var, r, s_rs):
                pool.wait_ge(s_var, n + 1)
                pool.tensor_tensor(r[:, :], var[:, :], mhalf[:, 0:NJ], ALU.pow).then_inc(s_rs, 1)

            for u in range(2):
                pool.wait_ge(s_yst[u], 16 * (E // 2))

            def first_pair(g):
                if after_first(g):
                    pool.wait_ge(s_comb, g)
                gather_indices(0, g, gi_s, wt_s)
                for n in range(2 * K):
                    gather_rows(0, n)

            first_pair(0)
            with pool.Fori(1, T) as g:
                first_pair(g)
            gather_indices(1, 0, gi0_s, wt0_s)
            pool.wait_ge(s_comb, T)
            gather_indices(1, 1, gi_s, wt_s)

            def first_rstd2(h):
                pool.wait_ge(s_var2h, h + 1)
                pool.tensor_tensor(rs2[:, 2 * h:2 * h + 2], ve2[:, 2 * h:2 * h + 2], mhalf[:, 0:2], ALU.pow).then_inc(s_rs2h, 1)

            first_rstd2(0)
            for u in range(2):
                pool.wait_ge(s_yst[u], 16 * (J // 2))
            for n in range(2 * K):
                gather_rows(1, n, gi0_s, GA0, s_ga0)
            for n in range(2 * K):
                gather_rows(1, n)
            first_rstd2(1)

            def group(g):
                ahead = live(g + 2) and live(g)
                if ahead:
                    pool.wait_ge(s_comb, T + g + 2)
                    gather_indices(1, g + 2, gi_s, wt_s)
                    if after_first(g):
                        gather_rows(1, 0)
                        gather_rows(1, 1)
                if live(g + 1):
                    if after_first(g):
                        pool.wait_ge(s_x2, g)
                    else:
                        pool.wait_ge(s_x2h, 2)
                    rstd(g, ve2, s_var2, rs2, s_rs2)
                if ahead:
                    if not after_first(g):
                        gather_rows(1, 0)
                        gather_rows(1, 1)
                    gather_rows(1, 2)
                if live(g - 2):
                    if after_first(g - 2):
                        pool.wait_ge(s_x4b, g - 2)
                    rstd(g - 2, ve4, s_var4, rs4, s_rs4)
                if ahead:
                    gather_rows(1, 3)
                if live(g - 1):
                    pool.wait_ge(s_x3, g)
                    if after_first(g - 1) and after_first(g - 2):
                        pool.wait_ge(s_h4, g - 2)
                    pool.tensor_tensor(x3b[:, bass.ds((g + 1) % 2, 1), :, :].rearrange("p o j d -> p (o j) d"), x3[:, :, :],
                                       b2_s[:, None, :].to_broadcast([P, NJ, D]), ALU.add).then_inc(s_x3b, 1)
                if live(g - 2):
                    pool.wait_ge(s_rs4, g - 1)
                    own.add(pool.tensor_tensor(mr4[:, :], mv4[:, 2:4, 0], rs4[:, 2:4], ALU.mult))
                    own.close()
                    pool.tensor_tensor(nb4[:, :], zeros[:, 0:2], mr4[:, :], ALU.subtract).then_inc(s_nb4, 1)
                if live(g):
                    rstd(g, ve3, s_var3, rs3, s_rs3)

            for g in range(2):
                group(g)
            with pool.Fori(2, T - 2) as g:
                group(g)
            for g in range(T - 2, T + 1):
                group(g)
            for h in range(2):
                cols = slice(2 * h, 2 * h + 2)
                pool.wait_ge(s_var4h, h + 1)
                pool.tensor_tensor(rs4[:, cols], ve4[:, cols], mhalf[:, 0:2], ALU.pow).then_inc(s_rs4h, 1)

        @block.scalar
        def _(act):
            def load_table(function):
                act.activation(warm[:, :], zeros[:, 0:1], function)

            def exps(g, t):
                act.wait_ge(s_max, g + 1)
                act.activation(prob[:, t % 2, :].rearrange("p (h n) -> p h n", h=2), PS[:, 2 * (t % 2):2 * (t % 2) + 2, :], ACT.Exp,
                               bias=nmax[:, t:t + 1], accum_out=rsum[:, t:t + 1]).then_inc(s_exp, 1)

            def x_high(b):
                act.wait_ge(s_xT, 16 * (b + 1))
                act.activation(xTh, xT_s[:, :], ACT.Copy).then_inc(s_xh, 1)

            def k_high(b):
                act.wait_ge(s_k_ev, b + 1)
                act.activation(KTh[:, :], KT[:, :], ACT.Copy).then_inc(s_kh, 1)

            def q_high(b, h):
                act.wait_ge(s_q_mm, 2 * b + h + 1)
                act.activation(QTh[:, h * 512:(h + 1) * 512], PS[:, 2 + h, :], ACT.Identity, bias=bq_s[:, 0:1]).then_inc(s_qh, 1)

            def v_out(b, h):
                act.wait_ge(s_v_mm, 2 * b + h + 1)
                act.activation(V[:, 4 * h:4 * h + 4, :], PS[:, 6 + h, :].rearrange("p (t d) -> p t d", t=4), ACT.Copy).then_inc(s_v_ev, 1)

            def router_out(r, n, dst, cols):
                act.wait_ge(s_r_mm, 4 * r + n + 1)
                act.activation(dst, PS[:, 7, 0:cols], ACT.Copy).then_inc(s_r_ev, 1)

            def router_exp(r):
                act.wait_ge(s_lsh, r + 1)
                act.activation(lex[:, :, :], lsh[:, :, :], ACT.Exp).then_inc(s_lex, 1)

            def body(b, first=False, last=False, extra=lambda t: None):
                for t in range(T):
                    g = b * T + t
                    if t == 4 and not first:
                        router_out(b - 1, 3, cnt[:, :, :].rearrange("p t e -> p (t e)"), T * E)
                    act.wait_ge(s_t, g + 1)
                    act.activation(PT[:, :, :].rearrange("p (h k) n -> p h (k n)", h=2), PS[:, 4:6, :], ACT.Copy).then_inc(s_e, 1)
                    if t == 1 and not first:
                        router_out(b - 1, 1, x1T[:, 512:1024], 512)
                    if t == 2 and not first:
                        router_exp(b - 1)
                    if t == 4 and not last:
                        x_high(b + 1)
                    if t == 6 and not last:
                        k_high(b + 1)
                    if t == 7 and not last:
                        q_high(b + 1, 0)
                        q_high(b + 1, 1)
                    if t + 2 < T:
                        exps(g + 2, t + 2)
                    if t == 0 and not first:
                        router_out(b - 1, 0, x1T[:, 0:512], 512)
                    if t == 1 and not first:
                        router_out(b - 1, 2, lg[:, :, :].rearrange("p t e -> p (t e)"), T * E)
                    extra(t)
                if not last:
                    exps(b * T + T, 0)
                    v_out(b + 1, 0)
                    exps(b * T + T + 1, 1)
                    v_out(b + 1, 1)

            for dst, src in ((bk_s, bk), (gm, gmask), (bq_s, bq)):
                act.dma_start(dst[:, :], src).then_inc(s_ldb, 16)
            act.wait_ge(s_init, 1)
            load_table(ACT.Exp)
            act.wait_ge(s_ldb, 16 * 3)
            k_high(0)
            q_high(0, 0)
            q_high(0, 1)
            v_out(0, 0)
            v_out(0, 1)
            exps(0, 0)
            exps(1, 1)
            act.wait_ge(s_ldw, 16 * 2)
            act.activation(wkh, wkT_s[:, :], ACT.Copy)
            act.activation(wqh, wqT_s[:, :], ACT.Copy).then_inc(s_kqh, 1)
            act.wait_ge(s_ld0, 16 * 4)
            body(0, first=True)
            with act.Fori(1, B - 1) as b:
                body(b)

            def slots_T(j, u):
                act.wait_ge(s_XT_mm, j + 1)
                act.activation(XTh[:, u, 0:512], PS[:, 0, :], ACT.Copy)
                act.activation(XTh[:, u, 512:SLOTS], PS[:, 1, 0:SLOTS - 512], ACT.Copy).then_inc(s_XTh, 1)

            def w13_high(j, u, n):
                act.wait_ge(s_w13[u], 16 * (n + 1))
                act.activation(w13h[:, u, :], w13_s[:, u, :], ACT.Copy).then_inc(s_wh, 1)

            def silu(j, k):
                act.wait_ge(s_ha, NU * j + k + 1)
                n = P if ORDER[k] < 6 else FT
                act.activation(sil[0:n, k % 3, :], PS[0:n, unit_bank(k), 0:HALF], ACT.Silu).then_inc(s_sil, 1)

            def results_out(j, u, stored):
                act.wait_ge(s_y, j + 1)
                if after_first(stored):
                    act.wait_ge(s_yst[u], 16 * stored)
                act.activation(Ys[:, u, 512:Q * D], PS[:, 7, 0:Q * D - 512], ACT.Copy).then_inc(s_ye1, 1)

            def pass_(j, u, m, between=lambda k: None, late=lambda: None):
                for k in range(2, NU):
                    silu(j, k)
                    between(k)
                if live(j + 1, J):
                    silu(j + 1, 0)
                    silu(j + 1, 1)
                if live(j + 2, J):
                    w13_high(j + 2, u, m + 1)
                    slots_T(j + 2, u)
                late()
                results_out(j, u, m)

            def ahead(t):
                if t == 5:
                    w13_high(0, 0, 0)
                if t == 6:
                    slots_T(0, 0)
                    w13_high(1, 1, 0)
                    load_table(ACT.Silu)
                if t == 7:
                    slots_T(1, 1)
                    silu(0, 0)

            def router_parts(k):
                if k == 4:
                    router_out(B - 1, 0, x1T[:, 0:512], 512)
                if k == 6:
                    router_out(B - 1, 1, x1T[:, 512:1024], 512)
                if k == 7:
                    router_out(B - 1, 2, lg[:, :, :].rearrange("p t e -> p (t e)"), T * E)

            def router_counts(k):
                if k == 7:
                    router_out(B - 1, 3, cnt[:, :, :].rearrange("p t e -> p (t e)"), T * E)

            def router_late():
                router_exp(B - 1)
                load_table(ACT.Silu)

            body(B - 1, last=True, extra=ahead)
            silu(0, 1)
            pass_(0, 0, 0)
            pass_(1, 1, 0, router_parts, router_late)
            pass_(2, 0, 1)
            pass_(3, 1, 1, router_counts)
            with act.Fori(2, J // 2 - 1) as i:
                pass_(2 * i, 0, i)
                pass_(2 * i + 1, 1, i)
            pass_(J - 2, 0, J // 2 - 1)
            pass_(J - 1, 1, J // 2 - 1)

            def gelu(g, c):
                act.wait_ge(s_f1, FC * g + c + 1)
                act.activation(H[:, c, :], PS[:, HIDDEN_BANKS[c], :], ACT.Gelu_apprx_tanh, bias=b1_s[:, c:c + 1]).then_inc(s_gelu, 1)

            def copy_out(mm, n, dst, bank, ev):
                act.wait_ge(mm, n)
                act.activation(dst, PS[:, bank, :].rearrange("p (k n) -> p k n", k=4), ACT.Copy).then_inc(ev, 1)

            def group(g):
                if live(g):
                    if after_first(g):
                        act.wait_ge(s_h3, g)
                    act.wait_ge(s_s3, g + 1)
                    act.activation(p3[:, :, :], PS[:, 2, :].rearrange("p (j n) -> p j n", j=NJ), ACT.Exp, scale=float(D) ** -0.5).then_inc(s_p3, 1)
                    copy_out(s_xv_mm, g + 1, xv[:, :, 0:D], 1, s_xv_ev)
                if live(g - 1):
                    copy_out(s_x3T_mm, g, x3Th[:, :].rearrange("p (k n) -> p k n", k=4), 0, s_x3Th)
                if live(g - 1):
                    for c in range(FC):
                        gelu(g - 1, c)
                if live(g + 1):
                    act.wait_ge(s_x2T_mm, g + 2)
                    act.activation(x2T[:, :, :].rearrange("p j (b s) -> p b j s", b=B), PS[:, 0, :].rearrange("p (b j s) -> p b j s", b=B, j=NJ),
                                   ACT.Copy).then_inc(s_x2T_ev, 1)
                if live(g - 2):
                    act.wait_ge(s_nb4, g - 1)
                    if after_first(g - 2):
                        act.wait_ge(s_out, 16 * B * (g - 2))
                    for j in (2, 3):
                        ins = act.activation(x4[:, j, :], h4[:, j, :], ACT.Identity, bias=nb4[:, j - 2:j - 1], scale=rs4[:, j:j + 1])
                    ins.then_inc(s_x4b, 1)

            load_table(ACT.Exp)
            act.activation(f1h[:, :], f1_s[:, :], ACT.Copy).then_inc(s_f1h, 1)
            for g in range(-1, 2):
                group(g)
            with act.Fori(2, T - 1) as g:
                group(g)
            for g in range(T - 1, T + 1):
                group(g)

        @block.vector
        def _(dve):
            own = Steps(dve, s_own)

            def k_out(b):
                dve.wait_ge(s_k_mm, b + 1)
                dve.scalar_tensor_tensor(out=KT[:, :].rearrange("p (h n) -> p h n", h=2), in0=PS[:, 0:2, :],
                                         scalar=bk_s[:, 0:1], in1=gm[:, :].rearrange("p (h n) -> p h n", h=2),
                                         op0=ALU.add, op1=ALU.mult).then_inc(s_k_ev, 1)

            def x_low(b):
                dve.wait_ge(s_xh, b)
                dve.tensor_tensor(xTl, xT_s[:, :], xTh.bitcast(F32), ALU.subtract).then_inc(s_xl, 1)

            def k_low(b):
                dve.wait_ge(s_kh, b + 1)
                dve.tensor_tensor(KTl[:, :], KT[:, :], KTh[:, :].bitcast(F32), ALU.subtract).then_inc(s_kl, 1)

            def q_low(b, h):
                dve.wait_ge(s_qh, 2 * b + h + 1)
                half = slice(h * 512, (h + 1) * 512)
                dve.scalar_tensor_tensor(out=QTl[:, half], in0=PS[:, 2 + h, :], scalar=bq_s[:, 0:1], in1=QTh[:, half].bitcast(F32),
                                         op0=ALU.add, op1=ALU.subtract).then_inc(s_ql, 1)

            def row_max(g, t):
                dve.wait_ge(s_s, g + 1)
                dve.tensor_reduce(nmax[:, t:t + 1], PS[:, 2 * (t % 2):2 * (t % 2) + 2, :], AX.XY, ALU.max, negate=True).then_inc(s_max, 1)

            def residual(g, t):
                dve.wait_ge(s_exp, g + 1)
                own.add(dve.reciprocal(rinv[:, t:t + 1], rsum[:, t:t + 1]))
                dve.wait_ge(s_pv, g + 1)
                own.wait()
                dve.scalar_tensor_tensor(out=h1[:, t, :], in0=PS[:, 6, 0:D], scalar=rinv[:, t:t + 1],
                                         in1=xb_s[:, t, :], op0=ALU.mult, op1=ALU.add).then_inc(s_o, 1)
                dve.wait_ge(s_o, g + 1)
                own.add(dve.bn_stats(st1[:, t, :], h1[:, t, :]))
                own.wait()
                own.add(dve.bn_aggr(mv1[:, t, :], st1[:, t, :]))

            def var1(b):
                own.wait()
                dve.tensor_scalar(ve1[:, :], mv1[:, :, 1], EPS, None, ALU.add).then_inc(s_var1, 1)

            def ln1(b, first=False):
                dve.wait_ge(s_rs1, b + 1)
                if not first:
                    dve.wait_ge(s_sc, 16 * K * T * b)
                    dve.wait_ge(s_x1all, 16 * b)
                for t in range(T):
                    ins = dve.tensor_scalar(x1b[:, t, :], h1[:, t, :], mv1[:, t, 0:1], rs1[:, t:t + 1], ALU.subtract, ALU.mult)
                ins.then_inc(s_x1, 1)

            def router_shift(r):
                dve.wait_ge(s_r_ev, 4 * r + 3)
                own.add(dve.tensor_reduce(lmx[:, :], lg[:, :, :], AX.X, ALU.max))
                own.wait()
                dve.tensor_tensor(lsh[:, :, :], lg[:, :, :], lmx[:, :, None].to_broadcast([P, T, E]), ALU.subtract).then_inc(s_lsh, 1)

            def router_probs(r):
                dve.wait_ge(s_lex, r + 1)
                own.add(dve.tensor_reduce(lsum[:, :], lex[:, :, :], AX.X, ALU.add))
                own.wait()
                own.add(dve.reciprocal(linv[:, :], lsum[:, :]))
                own.wait()
                own.add(dve.tensor_tensor(pr[:, :, :], lex[:, :, :], linv[:, :, None].to_broadcast([P, T, E]), ALU.mult))
                own.wait()

            def router_two(r):
                for t in range(T):
                    own.add(dve.max(top[:, t, :], pr[:, t, :]))
                for t in range(T):
                    own.wait(back=T - 1)
                    own.add(dve.max_index(tix[:, t, :], top[:, t, :], pr[:, t, :]))
                own.wait()
                own.add(dve.tensor_copy(tixf[:, :, :], tix[:, :, 0:K].rearrange("p t k -> p k t")))

            def router_choice(r):
                own.wait()
                own.add(dve.tensor_tensor(oh[:, :, :, :].rearrange("p k t e -> p (k t) e"),
                                          tixf[:, :, :].rearrange("p k t -> p (k t)")[:, :, None].to_broadcast([P, K * T, E]),
                                          iota[:, None, :].to_broadcast([P, K * T, E]), ALU.is_equal))
                own.wait()
                own.add(dve.tensor_tensor(both[:, 4:, :], oh[:, 0, :, :], oh[:, 1, :, :], ALU.add))
                own.add(dve.scalar_tensor_tensor(out=row_g[:, :], in0=tixf[:, :, :].rearrange("p k t -> p (k t)"), scalar=float(SLOTS),
                                                 in1=base_tab[:, r, :], op0=ALU.mult, op1=ALU.add))
                own.wait(back=1)
                own.add(dve.tensor_tensor(upto[:, 0, 4:, :], both[:, 4:, :], both[:, 3:-1, :], ALU.add))
                own.wait(back=1)
                own.add(dve.tensor_tensor(row_d[:, :], row_g[:, :], trash_tab[:, r, :], ALU.subtract))
                own.wait(back=1)
                own.add(dve.tensor_tensor(upto[:, 1, 4:, :], upto[:, 0, 4:, :], upto[:, 0, 2:-2, :], ALU.add))
                own.wait()
                dve.tensor_tensor(upto[:, 0, 4:, :], upto[:, 1, 4:, :], upto[:, 1, 0:-4, :], ALU.add).then_inc(s_both, 1)

            def router_rows(r):
                dve.wait_ge(s_r_ev, 4 * r + 4)
                own.add(dve.tensor_tensor(ohc[:, :, :, :], oh[:, :, :, :], cnt[:, None, :, :].to_broadcast([P, K, T, E]), ALU.mult))
                own.wait()
                own.add(dve.tensor_reduce(pos[:, :], ohc[:, :, :, :].rearrange("p k t e -> p (k t) e"), AX.X, ALU.add))
                own.wait()
                own.add(dve.scalar_tensor_tensor(out=row_s[:, :], in0=pos[:, :], scalar=float(CAP), in1=row_d[:, :], op0=ALU.min, op1=ALU.add))
                dve.scalar_tensor_tensor(out=gidx[:, r, :], in0=pos[:, :], scalar=float(CAP), in1=row_g[:, :], op0=ALU.min, op1=ALU.add)
                dve.scalar_tensor_tensor(out=wts[:, r, :].rearrange("p (k t) -> p k t", k=K), in0=pos[:, :].rearrange("p (k t) -> p k t", k=K),
                                         scalar=float(CAP), in1=top[:, :, 0:K].rearrange("p t k -> p k t"), op0=ALU.is_le, op1=ALU.mult)
                own.wait()
                own.add(dve.scalar_tensor_tensor(out=row_t[:, :], in0=pos[:, :], scalar=float(CAP), in1=row_s[:, :], op0=ALU.is_le, op1=ALU.mult))
                own.wait()
                dve.tensor_tensor(sidx[:, :], row_t[:, :], trash_tab[:, r, :], ALU.add).then_inc(s_idx, 1)

            def body(b, first=False, last=False, extra=lambda t: None):
                for t in range(T):
                    g = b * T + t
                    if t == 5 and not last:
                        x_low(b + 1)
                    if t == 6 and not last:
                        k_out(b + 1)
                    if t == 7 and not last:
                        k_low(b + 1)
                        q_low(b + 1, 0)
                        q_low(b + 1, 1)
                    if t == 2 and not first:
                        router_probs(b - 1)
                    if t == 4 and not first:
                        router_rows(b - 1)
                    if t + 2 < T:
                        row_max(g + 2, t + 2)
                    if t == 3 and not first:
                        router_choice(b - 1)
                    if t == 0:
                        dve.wait_ge(s_xb, b + 1)
                    extra(t)
                    residual(g, t)
                    if t == 1 and not first:
                        router_shift(b - 1)
                    if t == 2 and not first:
                        router_two(b - 1)
                var1(b)
                if not last:
                    row_max(b * T + T, 0)
                    row_max(b * T + T + 1, 1)
                if not last:
                    ln1(b, first)
                    own.close()

            dve.wait_ge(s_ldv, 16 * 4)
            dve.tensor_copy(bv_wide[:, :], bv_s[:, 0:1].to_broadcast([P, P])).then_inc(s_bvw, 1)
            dve.wait_ge(s_ldb, 16 * 3)
            k_out(0)
            dve.wait_ge(s_prep_mm, 1)
            dve.tensor_copy(wvoT_s[:, :], PS[:, 6, 0:D]).then_inc(s_prep_ev, 1)
            dve.wait_ge(s_prep_mm, 2)
            dve.tensor_tensor(beff[:, :], PS[:, 7, 0:D], bo_s[:, :], ALU.add).then_inc(s_prep_ev, 1)
            k_low(0)
            q_low(0, 0)
            q_low(0, 1)
            row_max(0, 0)
            row_max(1, 1)
            dve.wait_ge(s_prep_mm, 3)
            dve.tensor_copy(f1_s[:, :], PS[:, 6, :]).then_inc(s_prep_ev, 1)
            dve.wait_ge(s_prep_mm, 4)
            dve.tensor_copy(f2_s[:, :, :], PS[:, 7, :].rearrange("p (c d) -> p c d", c=FC)).then_inc(s_prep_ev, 1)
            dve.wait_ge(s_kqh, 1)
            dve.tensor_tensor(wkl, wkT_s[:, :], wkh.bitcast(F32), ALU.subtract)
            dve.tensor_tensor(wql, wqT_s[:, :], wqh.bitcast(F32), ALU.subtract).then_inc(s_kql, 1)
            dve.wait_ge(s_ld0, 16 * 4)
            body(0, first=True)
            with dve.Fori(1, B - 1) as b:
                body(b)

            def gated(j, u, k):
                dve.wait_ge(s_sil, NU * j + k + 1)
                c, h = ORDER[k] // 2, ORDER[k] % 2
                if c < 3:
                    dve.wait_ge(s_h, 6 * j + FULL[k])
                    dve.tensor_tensor(G[:, u, c, h * HALF:(h + 1) * HALF], sil[:, k % 3, :], PS[:, unit_bank(k) + 1, 0:HALF],
                                      ALU.mult).then_inc(s_g, 1)
                else:
                    dve.tensor_tensor(G[0:FT, u, c, h * HALF:(h + 1) * HALF], sil[0:FT, k % 3, :], PS[FT:2 * FT, unit_bank(k), 0:HALF],
                                      ALU.mult).then_inc(s_g, 1)

            def combine(pair, g, rows=GA, wt=wt_s, apart=False):
                if apart:
                    dve.wait_ge(s_ga0, 16 * 2 * K)
                else:
                    dve.wait_ge(s_ga, 16 * 2 * K * (pair * (T - 1) + g + 1))
                for k in range(K):
                    for b in range(2):
                        h = x1_all[:, bass.ds((2 * pair + b) * T + g, 1), :].rearrange("p o d -> p (o d)")
                        if k:
                            own.wait(back=1 - b)
                        ins = dve.scalar_tensor_tensor(out=h, in0=rows[:, K * b + k, :], scalar=wt[:, K * b + k:K * b + k + 1], in1=h,
                                                       op0=ALU.mult, op1=ALU.add)
                        if k == 0:
                            own.add(ins)
                ins.then_inc(s_comb, 1)

            def w13_low(j, u):
                dve.wait_ge(s_wh, j + 1)
                dve.tensor_tensor(w13l[:, u, :], w13_s[:, u, :], w13h[:, u, :].bitcast(F32), ALU.subtract).then_inc(s_wl, 1)

            def slots_low(j, u):
                dve.wait_ge(s_XTh, j + 1)
                dve.tensor_tensor(XTl[:, u, 0:512], PS[:, 0, :], XTh[:, u, 0:512].bitcast(F32), ALU.subtract)
                dve.tensor_tensor(XTl[:, u, 512:SLOTS], PS[:, 1, 0:SLOTS - 512], XTh[:, u, 512:SLOTS].bitcast(F32), ALU.subtract).then_inc(s_XTl, 1)

            def pass_(j, u, stored, between=lambda k: None, late=lambda: None):
                for k in range(2, NU):
                    gated(j, u, k)
                    between(k)
                if live(j + 1, J):
                    gated(j + 1, 1 - u, 0)
                    gated(j + 1, 1 - u, 1)
                if live(j + 2, J):
                    w13_low(j + 2, u)
                    slots_low(j + 2, u)
                late()
                dve.wait_ge(s_y, j + 1)
                if after_first(stored):
                    dve.wait_ge(s_yst[u], 16 * stored)
                dve.tensor_copy(Ys[:, u, 0:512], PS[:, 6, :]).then_inc(s_ye, 1)

            def ln1_late():
                ln1(B - 1)

            def choice_late():
                router_probs(B - 1)
                router_two(B - 1)
                router_choice(B - 1)

            def rows_late():
                router_rows(B - 1)

            def router_late():
                router_shift(B - 1)

            def ahead(t):
                if t == 6:
                    w13_low(0, 0)
                    slots_low(0, 0)
                if t == 7:
                    w13_low(1, 1)
                    slots_low(1, 1)
                    gated(0, 0, 0)

            body(B - 1, last=True, extra=ahead)
            gated(0, 0, 1)
            pass_(0, 0, 0, late=ln1_late)
            pass_(1, 1, 0, late=router_late)
            pass_(2, 0, 1, late=choice_late)
            pass_(3, 1, 1, late=rows_late)
            own.close()
            with dve.Fori(2, E // 2) as i:
                pass_(2 * i, 0, i)
                pass_(2 * i + 1, 1, i)
            dve.wait_ge(s_x1all, 16 * B)

            def pass_and_combine(i, u):
                pass_(2 * i + u, u, i, late=lambda: combine(0, 2 * (i - E // 2) + u))

            with dve.Fori(E // 2, J // 2 - 1) as i:
                pass_and_combine(i, 0)
                pass_and_combine(i, 1)
                own.close()
            pass_and_combine(J // 2 - 1, 0)
            pass_and_combine(J // 2 - 1, 1)
            own.close()

            def stats(h, st, mv, ve, s_var, js=range(NJ)):
                for j in js:
                    own.add(dve.bn_stats(st[:, j, :], h(j)))
                for j in js:
                    own.wait(back=len(js) - 1)
                    own.add(dve.bn_aggr(mv[:, j, :], st[:, j, :]))
                own.wait()
                dve.tensor_scalar(ve[:, js[0]:js[-1] + 1], mv[:, js[0]:js[-1] + 1, 1], EPS, None, ALU.add).then_inc(s_var, 1)

            def normal(h, mv, rs, xo, s_x, js=range(NJ)):
                for j in js:
                    ins = dve.tensor_scalar(xo[:, j, :], h[:, j, :], mv[:, j, 0:1], rs[:, j:j + 1], ALU.subtract, ALU.mult)
                ins.then_inc(s_x, 1)

            def x3T_low(g):
                dve.wait_ge(s_x3Th, g + 1)
                dve.tensor_tensor(x3Tl[:, :], PS[:, 0, :], x3Th[:, :].bitcast(F32), ALU.subtract).then_inc(s_x3Tl, 1)

            def group(g):
                if live(g + 1):
                    combine(1, g + 1)
                if live(g - 1):
                    dve.wait_ge(s_rs3, g)
                    if after_first(g - 1):
                        dve.wait_ge(s_x3b, g - 1)
                    normal(h3, mv3, rs3, x3, s_x3)
                if live(g + 1):
                    dve.wait_ge(s_comb, T + g + 2)
                    if after_first(g):
                        dve.wait_ge(s_x2, g)
                    else:
                        dve.wait_ge(s_x2h, 2)
                    stats(lambda b: x1_all[:, bass.ds(b * T + g + 1, 1), :].rearrange("p o d -> p (o d)"), st2, mv2, ve2, s_var2)
                if live(g - 1) and not live(g - 2):
                    x3T_low(g - 1)
                if live(g - 2):
                    dve.wait_ge(s_f2, g - 1)
                    if after_first(g - 2):
                        dve.wait_ge(s_x4, g - 2)
                        dve.wait_ge(s_x4b, g - 2)
                    dve.wait_ge(s_x3b, g - 1)
                    dve.tensor_tensor(h4[:, :, :], PS[:, 7, :].rearrange("p (j d) -> p j d", j=NJ),
                                      x3b[:, bass.ds(g % 2, 1), :, :].rearrange("p o j d -> p (o j) d"), ALU.add).then_inc(s_h4, 1)
                    dve.wait_ge(s_h4, g - 1)
                    if live(g - 1):
                        x3T_low(g - 1)
                    stats(lambda j: h4[:, j, :], st4, mv4, ve4, s_var4)
                if live(g + 1):
                    dve.wait_ge(s_rs2, g + 1)
                    dve.wait_ge(s_x2T_mm, g + 1)
                    for b in range(B):
                        ins = dve.tensor_scalar(x2[:, b, :], x1_all[:, bass.ds(b * T + g + 1, 1), :].rearrange("p o d -> p (o d)"),
                                                mv2[:, b, 0:1], rs2[:, b:b + 1], ALU.subtract, ALU.mult)
                    ins.then_inc(s_x2, 1)
                if live(g):
                    dve.wait_ge(s_pv3, g + 1)
                    own.add(dve.reciprocal(inv3[:, :].rearrange("p (h j) -> p h j", h=2), PS[:, 3:5, 0:2 * (D + 1)].rearrange("p h (j n) -> p h j n", j=2)[:, :, :, D]))
                    own.wait()
                    for j in range(NJ):
                        ins = dve.scalar_tensor_tensor(out=h3[:, j, :], in0=PS[:, 3 + j // 2, (j % 2) * (D + 1):(j % 2) * (D + 1) + D],
                                                       scalar=inv3[:, j:j + 1], in1=xv[:, j, 0:D], op0=ALU.mult, op1=ALU.add)
                    ins.then_inc(s_h3, 1)
                    dve.wait_ge(s_h3, g + 1)
                    stats(lambda j: h3[:, j, :], st3, mv3, ve3, s_var3)
                if live(g - 2):
                    dve.wait_ge(s_rs4, g - 1)
                    if after_first(g - 2):
                        dve.wait_ge(s_out, 16 * B * (g - 2))
                    normal(h4, mv4, rs4, x4, s_x4, range(2))
                own.close()

            for h in range(2):
                if h:
                    dve.tensor_copy(far_ident, ident)
                    dve.tensor_scalar(far.rearrange("p (j n) -> p j n", j=NJ), blockmask[:, None, :].to_broadcast([P, NJ, P]),
                                      1.0, -FAR, ALU.subtract, ALU.mult).then_inc(s_far, 1)
                    dve.wait_ge(s_f1h, 1)
                    dve.tensor_tensor(f1l[:, :], f1_s[:, :], f1h[:, :].bitcast(F32), ALU.subtract).then_inc(s_f1l, 1)
                    combine(1, 0, GA0, wt0_s, apart=True)
                    dve.wait_ge(s_comb, T + 1)
                bs = range(2 * h, 2 * h + 2)
                stats(lambda b: x1_all[:, b * T, :], st2, mv2, ve2, s_var2h, bs)
                dve.wait_ge(s_rs2h, h + 1)
                for b in bs:
                    ins = dve.tensor_scalar(x2[:, b, :], x1_all[:, b * T, :], mv2[:, b, 0:1], rs2[:, b:b + 1], ALU.subtract, ALU.mult)
                ins.then_inc(s_x2h, 1)
            for g in range(2):
                group(g)
            with dve.Fori(2, T - 1) as g:
                group(g)
            for g in range(T - 1, T + 1):
                group(g)
            dve.wait_ge(s_x4, T - 1)
            dve.wait_ge(s_x4b, T - 1)
            dve.wait_ge(s_x3b, T)
            for h in range(2):
                js = range(2 * h, 2 * h + 2)
                dve.wait_ge(s_f2h, h + 1)
                dve.tensor_tensor(h4[:, 2 * h:2 * h + 2, :], PS[:, (7, 2)[h], 2 * h * D:(2 * h + 2) * D].rearrange("p (j d) -> p j d", j=2),
                                  x3b[:, (T + 1) % 2, 2 * h:2 * h + 2, :], ALU.add).then_inc(s_h4h, 1)
                dve.wait_ge(s_h4h, h + 1)
                stats(lambda j: h4[:, j, :], st4, mv4, ve4, s_var4h, js)
            dve.wait_ge(s_out, 16 * B * (T - 1))
            for h in range(2):
                dve.wait_ge(s_rs4h, h + 1)
                normal(h4, mv4, rs4, x4, s_x4h, range(2 * h, 2 * h + 2))
            own.close()

        @block.tensor
        def _(pe):
            def split_product(out, wh, wl, h):
                cols = slice(h * 512, (h + 1) * 512)
                pe.matmul(out, wh, xTh[:, cols], start=True, stop=False)
                pe.matmul(out, wh, xTl[:, cols], start=False, stop=False)
                return pe.matmul(out, wl, xTh[:, cols], start=False, stop=True)

            def k_mm(b):
                if after_first(b):
                    pe.wait_ge(s_kql, 1)
                    pe.wait_ge(s_xl, b)
                else:
                    pe.wait_ge(s_xT, 16)
                for h in range(2):
                    if after_first(b):
                        mm = split_product(PS[:, h, :], wkh, wkl, h)
                    else:
                        mm = pe.matmul(PS[:, h, :], wkT_s[:, :], xT_s[:, h * 512:(h + 1) * 512], start=True, stop=True)
                mm.then_inc(s_k_mm, 1)

            def q_mm(b):
                for h in range(2):
                    if after_first(b):
                        mm = split_product(PS[:, 2 + h, :], wqh, wql, h)
                    else:
                        mm = pe.matmul(PS[:, 2 + h, :], wqT_s[:, :], xT_s[:, h * 512:(h + 1) * 512], start=True, stop=True)
                    mm.then_inc(s_q_mm, 1)

            def v_mm(b):
                for h in range(2):
                    for t in range(4):
                        mm = pe.matmul(PS[:, 6 + h, t * D:(t + 1) * D], xT_s[:, (4 * h + t) * P:(4 * h + t + 1) * P], wvoT_s[:, :],
                                       start=True, stop=True)
                    mm.then_inc(s_v_mm, 1)

            def scores(g, t):
                q = slice(t * P, (t + 1) * P)
                for h in range(2):
                    out, k = PS[:, 2 * (t % 2) + h, :], slice(h * 512, (h + 1) * 512)
                    pe.matmul(out, QTh[:, q], KTh[:, k], start=True, stop=False)
                    pe.matmul(out, QTh[:, q], KTl[:, k], start=False, stop=False)
                    mm = pe.matmul(out, QTl[:, q], KTh[:, k], start=False, stop=True)
                mm.then_inc(s_s, 1)

            def first_scores(b):
                pe.wait_ge(s_kl, b + 1)
                pe.wait_ge(s_ql, 2 * b + 1)
                scores(b * T, 0)
                pe.wait_ge(s_ql, 2 * b + 2)
                scores(b * T + 1, 1)

            def router_turn(r, h):
                if h == 0:
                    pe.wait_ge(s_x1, r + 1)
                if not isinstance(r, int) or r or h:
                    pe.wait_ge(s_r_ev, 4 * r + h)
                else:
                    pe.wait_ge(s_prep_ev, 4)
                for t in range(4):
                    mm = pe.transpose(PS[:, 7, t * P:(t + 1) * P], x1b[:, 4 * h + t, :], ident)
                mm.then_inc(s_r_mm, 1)

            def router_logits(r):
                pe.wait_ge(s_r_ev, 4 * r + 2)
                for t in range(T):
                    mm = pe.matmul(PS[:, 7, t * E:(t + 1) * E], x1T[:, t * P:(t + 1) * P], gateT_s[:, :], start=True, stop=True)
                mm.then_inc(s_r_mm, 1)

            def router_count(r):
                pe.wait_ge(s_both, r + 1)
                pe.matmul(PS[:, 7, 0:T * E], tri, both[:, 4:, :].rearrange("p t e -> p (t e)"), start=True, stop=False)
                pe.matmul(PS[:, 7, E:T * E], ones, upto[:, 0, 4:-1, :].rearrange("p t e -> p (t e)"), start=False, stop=True).then_inc(s_r_mm, 1)

            def body(b, first=False, last=False, extra=lambda t: None):
                for t in range(T):
                    g = b * T + t
                    pe.wait_ge(s_exp, g + 1)
                    if not (first and t == 0):
                        pe.wait_ge(s_e, g)
                    for k in range(T):
                        mm = pe.transpose(PS[:, 4 + k // 4, (k % 4) * P:(k % 4 + 1) * P], prob[:, t % 2, k * P:(k + 1) * P], ident)
                    mm.then_inc(s_t, 1)
                    if t == 1 and not first:
                        router_turn(b - 1, 1)
                    if t == 4 and not first:
                        router_count(b - 1)
                    if t == 6 and not last:
                        k_mm(b + 1)
                    extra(t)
                    if t == 7 and not last:
                        q_mm(b + 1)
                    if t + 2 < T:
                        scores(g + 2, t + 2)
                    if t == 0:
                        pe.wait_ge(s_v_ev, 2 * b + 2)
                    if t == 1 and not first:
                        router_logits(b - 1)
                    pe.wait_ge(s_e, g + 1)
                    if not (first and t == 0):
                        pe.wait_ge(s_o, g)
                    for k in range(T):
                        mm = pe.matmul(PS[:, 6, 0:D], PT[:, k, :], V[:, k, :], start=(k == 0), stop=(k == T - 1))
                    mm.then_inc(s_pv, 1)
                    if t == 0 and not first:
                        router_turn(b - 1, 0)
                if not last:
                    first_scores(b + 1)
                    pe.wait_ge(s_o, T * b + T)
                    if not first:
                        pe.wait_ge(s_r_ev, 4 * b)
                    v_mm(b + 1)

            pe.wait_ge(s_ldw, 16 * 2)
            k_mm(0)
            pe.wait_ge(s_ldv, 16 * 4)
            pe.matmul(PS[:, 6, 0:D], wv_s[:, :], woT_s[:, :], start=True, stop=True).then_inc(s_prep_mm, 1)
            pe.wait_ge(s_bvw, 1)
            pe.matmul(PS[:, 7, 0:D], bv_wide[:, :], woT_s[:, :], start=True, stop=True).then_inc(s_prep_mm, 1)
            q_mm(0)
            pe.wait_ge(s_prep_ev, 2)
            v_mm(0)
            first_scores(0)
            pe.wait_ge(s_ld1, 64)
            pe.wait_ge(s_v_ev, 2)
            pe.matmul(PS[:, 6, :], u1T_s[:, :], v1_s[:, :], start=True, stop=True).then_inc(s_prep_mm, 1)
            for c in range(FC):
                mm = pe.matmul(PS[:, 7, c * D:(c + 1) * D], u2T_s[:, c * P:(c + 1) * P], v2_s[:, :], start=True, stop=True)
            mm.then_inc(s_prep_mm, 1)
            pe.wait_ge(s_prep_ev, 4)
            pe.wait_ge(s_ld0, 16 * 4)
            body(0, first=True)
            with pe.Fori(1, B - 1) as b:
                body(b)

            def slots_T(j, u, n):
                pe.wait_ge(s_Xn[u], 16 * (n + 1))
                for q in range(Q):
                    mm = pe.transpose(PS[:, q // 4, (q % 4) * P:(q % 4 + 1) * P], Xn[:, u, q * D:(q + 1) * D], ident)
                mm.then_inc(s_XT_mm, 1)

            def unit(j, u, k, n, first=False):
                if k == 0:
                    pe.wait_ge(s_XTl, j + 1)
                    pe.wait_ge(s_wl, j + 1)
                if not first:
                    if k < 2:
                        pe.wait_ge(s_g, NU * j + k - 1)
                    elif k > 2:
                        pe.wait_ge(s_g, NU * j + k - 2)
                    elif live(j + 1, J):
                        pe.wait_ge(s_XTl, j + 2)
                c, h = ORDER[k] // 2, ORDER[k] % 2
                cols = slice(h * HALF, (h + 1) * HALF)
                xh, xl = XTh[:, u, cols], XTl[:, u, cols]

                def product(bank, chunk):
                    w = slice(chunk * P, (chunk + 1) * P)
                    pe.matmul(PS[:, bank, 0:HALF], w13h[:, u, w], xh, start=True, stop=False)
                    pe.matmul(PS[:, bank, 0:HALF], w13h[:, u, w], xl, start=False, stop=False)
                    return pe.matmul(PS[:, bank, 0:HALF], w13l[:, u, w], xh, start=False, stop=True)

                bank = unit_bank(k)
                product(bank, c).then_inc(s_ha, 1)
                if c < 3:
                    product(bank + 1, 4 + c).then_inc(s_h, 1)

            def down(j, u, n, first=False):
                pe.wait_ge(s_w[u], 32 * (n + 1))
                pe.wait_ge(s_g, NU * (j + 1))
                if not first:
                    pe.wait_ge(s_ye, j)
                    pe.wait_ge(s_ye1, j)
                for q in range(Q):
                    for c in range(4):
                        n = P if c < 3 else FT
                        mm = pe.matmul(PS[:, 6 + q // 4, (q % 4) * D:(q % 4 + 1) * D], G[0:n, u, c, q * P:(q + 1) * P], w2_s[0:n, u, c, :],
                                       start=(c == 0), stop=(c == 3))
                mm.then_inc(s_y, 1)

            def pass_(j, u, n, first=False, between=lambda k: None, routed=0):
                m = n + (1 if u else 0)
                for k in range(2, NU):
                    unit(j, u, k, n)
                    between(k)
                if live(j + 2, J):
                    pe.wait_ge(s_g, NU * j + 6)
                    slots_T(j + 2, u, n + 1)
                if live(j + 1, J):
                    unit(j + 1, 1 - u, 0, m)
                    unit(j + 1, 1 - u, 1, m)
                if routed:
                    pe.wait_ge(s_r_ev, routed)
                down(j, u, n, first)

            def ahead(t):
                if t == 6:
                    slots_T(0, 0, 0)
                if t == 7:
                    pe.wait_ge(s_XTl, 1)
                    slots_T(1, 1, 0)
                    unit(0, 0, 0, 0, first=True)

            def router_parts(k):
                if k in (3, 5):
                    pe.wait_ge(s_ye1, 1)
                    router_turn(B - 1, (k - 3) // 2)
                if k == 7:
                    router_logits(B - 1)

            def router_counts(k):
                if k == 7:
                    pe.wait_ge(s_ye1, 3)
                    router_count(B - 1)

            body(B - 1, last=True, extra=ahead)
            pe.wait_ge(s_e, B * T)
            unit(0, 0, 1, 0, first=True)
            pass_(0, 0, 0, first=True)
            pass_(1, 1, 0, between=router_parts, routed=4 * B - 1)
            pass_(2, 0, 1)
            pass_(3, 1, 1, between=router_counts, routed=4 * B)
            with pe.Fori(2, J // 2 - 1) as i:
                pass_(2 * i, 0, i)
                pass_(2 * i + 1, 1, i)
            pass_(J - 2, 0, J // 2 - 1)
            pass_(J - 1, 1, J // 2 - 1)

            def ffn_up(g):
                pe.wait_ge(s_f1l, 1)
                pe.wait_ge(s_x3Th, g + 1)
                for c in range(FC):
                    out, w = PS[:, HIDDEN_BANKS[c], :], slice(c * P, (c + 1) * P)
                    pe.matmul(out, f1h[:, w], x3Th[:, :], start=True, stop=False)
                    pe.matmul(out, f1l[:, w], x3Th[:, :], start=False, stop=False)
                    if c == EARLY - 1:
                        pe.wait_ge(s_x3Tl, g + 1)
                        for d in range(EARLY):
                            pe.matmul(PS[:, HIDDEN_BANKS[d], :], f1h[:, d * P:(d + 1) * P], x3Tl[:, :], start=False, stop=True).then_inc(s_f1, 1)
                    if c >= EARLY:
                        pe.matmul(out, f1h[:, w], x3Tl[:, :], start=False, stop=True).then_inc(s_f1, 1)

            def ffn_down(g, h, bank=7):
                if h == 0:
                    pe.wait_ge(s_gelu, FC * g + FC)
                    if after_first(g):
                        pe.wait_ge(s_h4, g)
                for j in (2 * h, 2 * h + 1):
                    for c in range(FC):
                        mm = pe.matmul(PS[:, bank, j * D:(j + 1) * D], H[:, c, j * P:(j + 1) * P], f2_s[:, c, :], start=(c == 0), stop=(c == FC - 1))
                return mm

            def attend(g):
                pe.wait_ge(s_p3, g + 1)
                pe.wait_ge(s_xv_ev, g + 1)
                for j in range(NJ):
                    mm = pe.matmul(PS[:, 3 + j // 2, (j % 2) * (D + 1):(j % 2 + 1) * (D + 1)], p3[:, j, :], xv[:, j, :], start=True, stop=True)
                mm.then_inc(s_pv3, 1)

            def group(g):
                if live(g - 2):
                    ffn_down(g - 2, 0)
                if live(g):
                    pe.wait_ge(s_x2T_ev, g + 1)
                    if not after_first(g):
                        pe.wait_ge(s_far, 1)
                    pe.matmul(PS[:, 2, :], far_ident, far, start=True, stop=False)
                    for j in range(NJ):
                        mm = pe.matmul(PS[:, 2, j * P:(j + 1) * P], x2T[:, j, :], x2T[:, j, :], start=False, stop=(j == NJ - 1))
                    mm.then_inc(s_s3, 1)
                    for j in range(NJ):
                        mm = pe.transpose(PS[:, 1, j * P:(j + 1) * P], x2T[:, j, :], ident)
                    mm.then_inc(s_xv_mm, 1)
                if live(g - 2):
                    ffn_down(g - 2, 1).then_inc(s_f2, 1)
                if live(g - 1):
                    pe.wait_ge(s_x3, g)
                    for j in range(NJ):
                        mm = pe.transpose(PS[:, 0, j * P:(j + 1) * P], x3[:, j, :], ident)
                    mm.then_inc(s_x3T_mm, 1)
                if live(g):
                    attend(g)
                if live(g - 1):
                    ffn_up(g - 1)
                if live(g + 1):
                    if after_first(g + 1):
                        pe.wait_ge(s_x2, g + 1)
                    for b in range(B):
                        if not after_first(g + 1) and b % 2 == 0:
                            pe.wait_ge(s_x2h, b // 2 + 1)
                        mm = pe.transpose(PS[:, 0, b * P:(b + 1) * P], x2[:, b, :], ident)
                    mm.then_inc(s_x2T_mm, 1)

            for g in range(-1, 2):
                group(g)
            with pe.Fori(2, T - 1) as g:
                group(g)
            for g in range(T - 1, T + 1):
                group(g)
            for h in range(2):
                ffn_down(T - 1, h, (7, 2)[h]).then_inc(s_f2h, 1)


def tables():
    c = np.zeros((P, C_END), np.float32)
    i = np.arange(P)
    c[:, C_ID:C_ID + P] = np.eye(P)
    c[:, C_TRI:C_TRI + P] = i[:, None] <= i[None, :]
    c[:, C_ONE:C_ONE + P] = 1
    c[:, C_BLK:C_BLK + P] = i[:, None] % SUB == i[None, :] % SUB
    b, k, t = np.meshgrid(np.arange(B), np.arange(K), np.arange(T), indexing="ij")
    c[:, C_BASE:C_TRASH] = ((b // 2) * E * SLOTS + (b % 2) * CAP - 1).reshape(1, -1)
    c[:, C_TRASH:C_IOTA] = ROWS + ((b * K + k) * T + t).reshape(1, -1) * P + i[:, None]
    c[:, C_IOTA:C_END] = np.arange(E)
    s = np.arange(S, dtype=np.float32)
    g = np.exp(np.float32(-0.5) * ((s - np.float32(S / 2)) / np.float32(S / 4)) ** 2) / np.sqrt(np.float32(D))
    return c, np.ascontiguousarray(np.broadcast_to(g.astype(np.float32)[None, :], (P, S)))


def kernel(**inputs):
    import concourse.bacc as _bacc
    from concourse.bass_utils import run_bass_kernel_spmd as _run

    def a(name):
        return np.asarray(inputs[name])

    consts, gmask = tables()
    x = a("L0_attn_x").reshape(B * S, D)
    w1, w3 = a("L0_ffn_w1"), a("L0_ffn_w3")
    laid = {
        "xT": x.T, "x": x,
        "wqT": a("L0_attn_Wq").T, "wkT": a("L0_attn_Wk").T, "wv": a("L0_attn_Wv"), "woT": a("L0_attn_Wo").T,
        "bq": a("L0_attn_bq").reshape(D, 1), "bk": a("L0_attn_bk").reshape(D, 1), "bv": a("L0_attn_bv").reshape(D, 1),
        "bo": np.broadcast_to(a("L0_attn_bo").reshape(1, D), (P, D)),
        "gateT": a("L0_ffn_gate_w").T,
        "w13": np.concatenate([w1, w3[:, :, 3 * P:], w3[:, :, :3 * P]], axis=2),
        "w2": a("L0_ffn_w2"),
        "u1T": a("L1_ffn_U1").T, "v1": a("L1_ffn_V1"), "u2T": a("L1_ffn_U2").T, "v2": a("L1_ffn_V2"),
        "b1": a("L1_ffn_b1").reshape(FC, P).T, "b2": np.broadcast_to(a("L1_ffn_b2").reshape(1, D), (P, D)),
        "consts": consts, "gmask": gmask,
    }
    nc = _bacc.Bacc("TRN2", target_bir_lowering=False, num_devices=1)
    arrays, args = {}, []
    for name, v in laid.items():
        v = np.ascontiguousarray(v)
        arrays[f"in_{name}"] = v
        args.append(nc.dram_tensor(f"in_{name}", v.shape, mybir.dt.from_np(v.dtype), kind="ExternalInput").ap())
    args.append(nc.dram_tensor("out_0", (B, S, D), F32, kind="ExternalOutput").ap())
    build(nc, *args)
    r = _run(nc, [arrays], core_ids=[0])
    return r.results[0]["out_0"]
```
